# Optimizing a Trainium2 kernel written in Bass

```python
import numpy as np
import jax
import jax.numpy as jnp

def _softmax(x, axis=-1):
    return jax.nn.softmax(x, axis=axis)

def _gelu(x):
    return jax.nn.gelu(x, approximate=True)

def _silu(x):
    return jax.nn.silu(x)

def _sigmoid(x):
    return jax.nn.sigmoid(x)

def _layernorm(x, axis=-1, eps=1e-05):
    m = jnp.mean(x, axis=axis, keepdims=True)
    v = jnp.var(x, axis=axis, keepdims=True)
    return (x - m) / jnp.sqrt(v + eps)

def _scatter_add(tgt, idx, src, axis=0):
    return tgt.at[idx].add(src)

def _segment_sum(src, seg, n):
    return jax.ops.segment_sum(src, seg, n)
kernel_name = 'mk_xattn_seq_d2_seqx_r8_cdd753'

def setup_inputs(seed: int=0):
    np.random.seed(seed)
    _w = jnp.asarray

    def _rec_inputs():
        import jax
        import jax.numpy as jnp
        _rk = jax.random.key(seed)
        x = -0.0002928 + 1 * jax.random.normal(jax.random.fold_in(_rk, 1), (8, 128, 256), jnp.float32)
        _lenS = 128 - jax.random.randint(jax.random.fold_in(_rk, 7), (8,), 0, max(1, 128 // 4) + 1, jnp.int32)
        _lenS2 = 128 - jax.random.randint(jax.random.fold_in(_rk, 8), (8,), 0, max(1, 128 // 4) + 1, jnp.int32)
        _ctx_2048P = jax.random.normal(jax.random.fold_in(_rk, 11), (8, 16, 256), jnp.float32)
        _ctx_2048c = jax.random.dirichlet(jax.random.fold_in(_rk, 511), 0.3 * jnp.ones((16,), jnp.float32), (8, 128))
        _ctx_2048t = jnp.einsum('bsk,bkd->bsd', _ctx_2048c, _ctx_2048P)
        _ctx_2048t = _ctx_2048t * jax.lax.rsqrt(jnp.mean(jnp.square(_ctx_2048t)) + 1e-12) * 0.953939
        ctx_2048 = 0.000189249 + 0.0999589 * (_ctx_2048t + 0.3 * jax.random.normal(jax.random.fold_in(_rk, 611), (8, 128, 256), jnp.float32))
        return (x, ctx_2048)
    x, ctx_2048 = _rec_inputs()

    def _L0_xattn_setup():
        import jax, jax.numpy as jnp
        import numpy as np
        B, L, E, H = (4, 64, 256, 32)
        S = E // H
        EXTRA_MAA, EXTRA_DECAY = (32, 64)
        EPS = 1e-05

        def _ln(x, w, b):
            m = jnp.mean(x, axis=-1, keepdims=True)
            v = jnp.mean((x - m) ** 2, axis=-1, keepdims=True)
            return (x - m) * jax.lax.rsqrt(v + EPS) * w + b

        def _token_shift(xn, prev_row):
            first = (prev_row - xn[:, 0])[:, None]
            rest = xn[:, :-1] - xn[:, 1:]
            return jnp.concatenate([first, rest], axis=1)
        key = jax.random.key(seed)
        ks = jax.random.split(key, 24)
        rn = lambda k, shp, s=1.0: jax.random.normal(k, shp, dtype=jnp.float32) * s
        return dict(x=rn(ks[0], (B, L, E)), state=rn(ks[1], (B, 2 + S, E), 0.1), ln1_w=jnp.ones((E,), jnp.float32), ln1_b=jnp.zeros((E,), jnp.float32), ln2_w=jnp.ones((E,), jnp.float32), ln2_b=jnp.zeros((E,), jnp.float32), maa_x=rn(ks[2], (E,), 0.02), maa_w1=rn(ks[3], (E, 5 * EXTRA_MAA), 0.02), maa_w2=rn(ks[4], (5, EXTRA_MAA, E), 0.02), maa_stack=rn(ks[5], (5, E), 0.02), time_decay=rn(ks[6], (E,), 0.5), decay_w1=rn(ks[7], (E, EXTRA_DECAY), 0.02), decay_w2=rn(ks[8], (EXTRA_DECAY, E), 0.02), faaaa=rn(ks[9], (H, S), 0.1), Wr=rn(ks[10], (E, E), 0.02), Wk=rn(ks[11], (E, E), 0.02), Wv=rn(ks[12], (E, E), 0.02), Wg=rn(ks[13], (E, E), 0.02), Wo=rn(ks[14], (E, E), 0.02), gn_w=jnp.ones((E,), jnp.float32), gn_b=jnp.zeros((E,), jnp.float32), ffn_maa_k=rn(ks[15], (E,), 0.02), ffn_maa_r=rn(ks[16], (E,), 0.02), ffn_Wk=rn(ks[17], (E, E), 0.02), ffn_Wr=rn(ks[18], (E, E), 0.02), ffn_Wv=rn(ks[19], (E, E), 0.02), i=0)
    _L0_xattn_all = _L0_xattn_setup()
    _L0_xattn_in = {k: v for k, v in _L0_xattn_all.items() if k in ('ln1_w', 'ln1_b', 'ln2_w', 'ln2_b', 'maa_x', 'maa_w1', 'maa_w2', 'maa_stack', 'time_decay', 'decay_w1', 'decay_w2', 'faaaa', 'Wr', 'Wk', 'Wv', 'Wg', 'Wo', 'gn_w', 'gn_b', 'ffn_maa_k', 'ffn_maa_r', 'ffn_Wk', 'ffn_Wr', 'ffn_Wv')}
    del _L0_xattn_all

    def _L1_xattn_setup():
        import jax, jax.numpy as jnp
        import numpy as np
        D_MODEL = 128
        N_HEAD = 16
        D_HEAD = 64
        IDX_LIST = [128, 256]
        SCALE = 1.0 / D_HEAD ** 0.5
        LN_EPS = 1e-05
        key = jax.random.key(seed)
        ks = jax.random.split(key, 9)
        s = 0.02
        B, L = (2, 256)
        return {'z1ss': jax.random.normal(ks[0], (B, D_MODEL, L), dtype=jnp.float32), 'u1ss': jax.random.normal(ks[1], (B, D_MODEL, L), dtype=jnp.float32), 'Wqkv0': jax.random.normal(ks[2], (3 * N_HEAD * D_HEAD, D_MODEL), dtype=jnp.float32) * s, 'Wqkv1': jax.random.normal(ks[3], (3 * N_HEAD * D_HEAD, D_MODEL), dtype=jnp.float32) * s, 'Winj0': jax.random.normal(ks[4], (3 * N_HEAD * D_HEAD, D_MODEL), dtype=jnp.float32) * s, 'Winj1': jax.random.normal(ks[5], (3 * N_HEAD * D_HEAD, D_MODEL), dtype=jnp.float32) * s, 'Wo': jax.random.normal(ks[6], (D_MODEL, N_HEAD * D_HEAD), dtype=jnp.float32) * s, 'bo': jax.random.normal(ks[7], (D_MODEL,), dtype=jnp.float32) * s, 'r_w_bias': jax.random.uniform(ks[8], (N_HEAD, D_HEAD), minval=-0.05, maxval=0.05, dtype=jnp.float32)}
    _L1_xattn_all = _L1_xattn_setup()
    _L1_xattn_in = {k: v for k, v in _L1_xattn_all.items() if k in ('Wqkv0', 'Wqkv1', 'Winj0', 'Winj1', 'Wo', 'bo', 'r_w_bias')}
    del _L1_xattn_all
    return {'x': x, 'ctx_2048': ctx_2048, 'L0_xattn_ln1_w': _L0_xattn_in['ln1_w'], 'L0_xattn_ln1_b': _L0_xattn_in['ln1_b'], 'L0_xattn_ln2_w': _L0_xattn_in['ln2_w'], 'L0_xattn_ln2_b': _L0_xattn_in['ln2_b'], 'L0_xattn_maa_x': _L0_xattn_in['maa_x'], 'L0_xattn_maa_w1': _L0_xattn_in['maa_w1'], 'L0_xattn_maa_w2': _L0_xattn_in['maa_w2'], 'L0_xattn_maa_stack': _L0_xattn_in['maa_stack'], 'L0_xattn_time_decay': _L0_xattn_in['time_decay'], 'L0_xattn_decay_w1': _L0_xattn_in['decay_w1'], 'L0_xattn_decay_w2': _L0_xattn_in['decay_w2'], 'L0_xattn_faaaa': _L0_xattn_in['faaaa'], 'L0_xattn_Wr': _L0_xattn_in['Wr'], 'L0_xattn_Wk': _L0_xattn_in['Wk'], 'L0_xattn_Wv': _L0_xattn_in['Wv'], 'L0_xattn_Wg': _L0_xattn_in['Wg'], 'L0_xattn_Wo': _L0_xattn_in['Wo'], 'L0_xattn_gn_w': _L0_xattn_in['gn_w'], 'L0_xattn_gn_b': _L0_xattn_in['gn_b'], 'L0_xattn_ffn_maa_k': _L0_xattn_in['ffn_maa_k'], 'L0_xattn_ffn_maa_r': _L0_xattn_in['ffn_maa_r'], 'L0_xattn_ffn_Wk': _L0_xattn_in['ffn_Wk'], 'L0_xattn_ffn_Wr': _L0_xattn_in['ffn_Wr'], 'L0_xattn_ffn_Wv': _L0_xattn_in['ffn_Wv'], 'L1_xattn_Wqkv0': _L1_xattn_in['Wqkv0'], 'L1_xattn_Wqkv1': _L1_xattn_in['Wqkv1'], 'L1_xattn_Winj0': _L1_xattn_in['Winj0'], 'L1_xattn_Winj1': _L1_xattn_in['Winj1'], 'L1_xattn_Wo': _L1_xattn_in['Wo'], 'L1_xattn_bo': _L1_xattn_in['bo'], 'L1_xattn_r_w_bias': _L1_xattn_in['r_w_bias']}

def reference(x, ctx_2048, L0_xattn_ln1_w, L0_xattn_ln1_b, L0_xattn_ln2_w, L0_xattn_ln2_b, L0_xattn_maa_x, L0_xattn_maa_w1, L0_xattn_maa_w2, L0_xattn_maa_stack, L0_xattn_time_decay, L0_xattn_decay_w1, L0_xattn_decay_w2, L0_xattn_faaaa, L0_xattn_Wr, L0_xattn_Wk, L0_xattn_Wv, L0_xattn_Wg, L0_xattn_Wo, L0_xattn_gn_w, L0_xattn_gn_b, L0_xattn_ffn_maa_k, L0_xattn_ffn_maa_r, L0_xattn_ffn_Wk, L0_xattn_ffn_Wr, L0_xattn_ffn_Wv, L1_xattn_Wqkv0, L1_xattn_Wqkv1, L1_xattn_Winj0, L1_xattn_Winj1, L1_xattn_Wo, L1_xattn_bo, L1_xattn_r_w_bias):
    import jax
    import jax.numpy as jnp

    def _L0_xattn_ref(x, state, ln1_w, ln1_b, ln2_w, ln2_b, maa_x, maa_w1, maa_w2, maa_stack, time_decay, decay_w1, decay_w2, faaaa, Wr, Wk, Wv, Wg, Wo, gn_w, gn_b, ffn_maa_k, ffn_maa_r, ffn_Wk, ffn_Wr, ffn_Wv, i):
        import jax, jax.numpy as jnp
        import numpy as np
        B, L, E, H = (4, 64, 256, 32)
        S = E // H
        EXTRA_MAA, EXTRA_DECAY = (32, 64)
        EPS = 1e-05

        def _ln(x, w, b):
            m = jnp.mean(x, axis=-1, keepdims=True)
            v = jnp.mean((x - m) ** 2, axis=-1, keepdims=True)
            return (x - m) * jax.lax.rsqrt(v + EPS) * w + b

        def _token_shift(xn, prev_row):
            first = (prev_row - xn[:, 0])[:, None]
            rest = xn[:, :-1] - xn[:, 1:]
            return jnp.concatenate([first, rest], axis=1)
        b, l = (x.shape[0], x.shape[1])
        i0 = (2 + S) * i + 0
        i1 = (2 + S) * i + 1
        xn = _ln(x, ln1_w, ln1_b)
        sx = _token_shift(xn, state[:, i1])
        xxx = jnp.tanh((xn + sx * maa_x) @ maa_w1).reshape(b, l, 5, 1, EXTRA_MAA)
        xxx = jnp.matmul(xxx, maa_w2).reshape(b, l, 5, E)
        x5 = xn[:, :, None] + sx[:, :, None] * (maa_stack + xxx)
        w = jnp.exp(-jnp.exp(time_decay + jnp.tanh(x5[:, :, 1] @ decay_w1) @ decay_w2))
        w = w.reshape(b, l, H, S)
        r = (x5[:, :, 3] @ Wr.T).reshape(b, l, H, S)
        k = (x5[:, :, 0] @ Wk.T).reshape(b, l, H, S)
        v = (x5[:, :, 2] @ Wv.T).reshape(b, l, H, S)
        g = jax.nn.silu(x5[:, :, 4] @ Wg.T)
        s0 = state[:, (2 + S) * i + 2:(2 + S) * (i + 1)].reshape(b, H, S, S)
        u = faaaa[None, :, :, None]

        def step(s, rkvw):
            r_t, k_t, v_t, w_t = rkvw
            a = k_t[:, :, :, None] * v_t[:, :, None, :]
            out = jnp.einsum('bhk,bhkd->bhd', r_t, u * a + s)
            return (a + w_t[:, :, :, None] * s, out)
        xs = tuple((jnp.moveaxis(t, 1, 0) for t in (r, k, v, w)))
        _, outs = jax.lax.scan(step, s0, xs)
        att = jnp.moveaxis(outs, 0, 1).reshape(b, l, E)
        a4 = att.reshape(b, l, H, S)
        m = jnp.mean(a4, axis=-1, keepdims=True)
        var = jnp.mean((a4 - m) ** 2, axis=-1, keepdims=True)
        att = ((a4 - m) * jax.lax.rsqrt(var + EPS)).reshape(b, l, E) * gn_w + gn_b
        x = x + att * g @ Wo.T
        xn2 = _ln(x, ln2_w, ln2_b)
        sx2 = _token_shift(xn2, state[:, i0])
        xk = xn2 + sx2 * ffn_maa_k
        xr = xn2 + sx2 * ffn_maa_r
        rr = jax.nn.sigmoid(xr @ ffn_Wr.T)
        kk = jnp.square(jax.nn.relu(xk @ ffn_Wk.T))
        x = x + rr * (kk @ ffn_Wv.T)
        return x

    def _L1_xattn_ref(z1ss, u1ss, Wqkv0, Wqkv1, Winj0, Winj1, Wo, bo, r_w_bias):
        import jax, jax.numpy as jnp
        import numpy as np
        D_MODEL = 128
        N_HEAD = 16
        D_HEAD = 64
        IDX_LIST = [128, 256]
        SCALE = 1.0 / D_HEAD ** 0.5
        LN_EPS = 1e-05
        bsz, d_model, qlen = z1ss.shape
        bounds = [0] + IDX_LIST
        Wq_list, Wi_list = ([Wqkv0, Wqkv1], [Winj0, Winj1])
        chunks = []
        for i in range(len(IDX_LIST)):
            s, e = (bounds[i], bounds[i + 1])
            h = jnp.einsum('od,bdl->bol', Wq_list[i], z1ss[:, :, s:e])
            h = h + jnp.einsum('od,bdl->bol', Wi_list[i], u1ss[:, :, s:e])
            chunks.append(h)
        w_heads = jnp.concatenate(chunks, axis=2)
        q, k, v = jnp.split(w_heads, 3, axis=1)
        q = q[:, :, -qlen:]
        klen = k.shape[2]
        q = q.reshape(bsz, N_HEAD, D_HEAD, qlen)
        k = k.reshape(bsz, N_HEAD, D_HEAD, klen)
        v = v.reshape(bsz, N_HEAD, D_HEAD, klen)
        rq = q + r_w_bias[None, :, :, None]
        score = jnp.einsum('bndi,bndj->bnij', rq, k) * SCALE
        prob = jax.nn.softmax(score, axis=-1)
        attn_vec = jnp.einsum('bnij,bndj->bndi', prob, v)
        attn_vec = attn_vec.reshape(bsz, N_HEAD * D_HEAD, qlen)
        attn_out = jnp.einsum('od,bdl->bol', Wo, attn_vec) + bo[None, :, None]
        x = attn_out + z1ss
        m = jnp.mean(x, axis=1, keepdims=True)
        var = jnp.var(x, axis=1, keepdims=True)
        return (x - m) * jax.lax.rsqrt(var + LN_EPS)
    x = _L0_xattn_ref(x, ctx_2048, L0_xattn_ln1_w, L0_xattn_ln1_b, L0_xattn_ln2_w, L0_xattn_ln2_b, L0_xattn_maa_x, L0_xattn_maa_w1, L0_xattn_maa_w2, L0_xattn_maa_stack, L0_xattn_time_decay, L0_xattn_decay_w1, L0_xattn_decay_w2, L0_xattn_faaaa, L0_xattn_Wr, L0_xattn_Wk, L0_xattn_Wv, L0_xattn_Wg, L0_xattn_Wo, L0_xattn_gn_w, L0_xattn_gn_b, L0_xattn_ffn_maa_k, L0_xattn_ffn_maa_r, L0_xattn_ffn_Wk, L0_xattn_ffn_Wr, L0_xattn_ffn_Wv, 0)
    x = _L1_xattn_ref(x, ctx_2048, L1_xattn_Wqkv0, L1_xattn_Wqkv1, L1_xattn_Winj0, L1_xattn_Winj1, L1_xattn_Wo, L1_xattn_bo, L1_xattn_r_w_bias)
    return x

_drawn_inputs = setup_inputs


def setup_inputs(seed=0):
    import zlib

    import numpy as np

    out = dict(_drawn_inputs(seed))
    spreads = {'L0_xattn_ln1_w': (1.0, 0.557),
     'L0_xattn_ln1_b': (0.0, 0.565),
     'L0_xattn_ln2_w': (1.0, 0.6),
     'L0_xattn_ln2_b': (0.0, 0.8),
     'L0_xattn_gn_w': (1.0, 0.6),
     'L0_xattn_gn_b': (0.0, 0.8)}
    factors = {'ctx_2048': 8.0,
     'L0_xattn_maa_x': 8.0,
     'L0_xattn_maa_w1': 6.857,
     'L0_xattn_maa_w2': 6.857,
     'L0_xattn_maa_stack': 8.0,
     'L0_xattn_time_decay': 2.753,
     'L0_xattn_decay_w1': 8.0,
     'L0_xattn_decay_w2': 8.0,
     'L0_xattn_faaaa': 5.497,
     'L0_xattn_ffn_maa_k': 8.0,
     'L0_xattn_ffn_maa_r': 8.0,
     'L0_xattn_ffn_Wk': 3.042,
     'L0_xattn_ffn_Wr': 8.0,
     'L0_xattn_ffn_Wv': 3.026,
     'L1_xattn_Wqkv0': 8.0,
     'L1_xattn_Wqkv1': 8.0,
     'L1_xattn_Winj0': 8.0,
     'L1_xattn_Winj1': 8.0,
     'L1_xattn_Wo': 6.293,
     'L1_xattn_r_w_bias': 8.0,
     'L1_xattn_bo': 46.609}
    for name, (base, spread) in spreads.items():
        noise = np.random.default_rng([zlib.crc32(name.encode()), seed]).standard_normal(out[name].shape)
        drawn = base * np.exp(spread * noise) if base else spread * noise
        out[name] = jnp.asarray(drawn.astype(out[name].dtype))
    for name, factor in factors.items():
        out[name] = (out[name] * factor).astype(out[name].dtype)
    return out
```

```python
from contextlib import ExitStack

import concourse.bass as bass
from concourse import mybir

F32 = mybir.dt.float32
ALU = mybir.AluOpType
ACT = mybir.ActivationFunctionType
AX = mybir.AxisListType

P = 128
B = 8
T = 128
E = 256
ET = E // P
SD = 8
HT = P // SD
H0 = E // SD
MIX = 5
XM = 32
XD = 64
EPS = 1e-5
NH = 16
DH = 64
NP = NH // 2
HD = NH * DH
SCALE = DH ** -0.5
VW = DH + 1

MIX_ORDER = [1, 0, 2, 3, 4]
SLOT_W, SLOT_K, SLOT_V, SLOT_R, SLOT_G = range(MIX)
MIX_USES = [("mix0", [0, 1]), ("mix1", [2, 3]), ("mix2", [4])]

CONSTS = [("ln1_w", ET), ("ln1_b", ET), ("ln2_w", ET), ("ln2_b", ET), ("maa_x", ET), ("maa", MIX * ET),
          ("decay", ET), ("bonus", ET), ("gn_w", ET), ("gn_b", ET), ("ffn_k", ET), ("ffn_r", ET),
          ("q_bias", NP), ("prev", 2 * B * ET)]
COL, _n = {}, 0
for _name, _w in CONSTS:
    COL[_name] = _n
    _n += _w
NCONST = _n

L0W = ["Wk", "Wr", "Wv", "Wg", "Wo", "fWk", "fWr", "fWv"]

L0_USES = ["xT", "mixin", "mix0", "mix1", "mix2", "dec1", "dec2", "kr", "vg", "vr0", "vr1", "vr2", "vr3",
           "red", "attT", "wo", "x2T", "kkrr", "ffn"]
STEP_USES = ["xT", "mixin", "mix0", "AT2'",
             "mix1", "mix2", "V00", "V01",
             "dec1", "AT3'", "dec2", "kr",
             "vg", "Y'", "vr0", "V10", "V11", "vr1",
             "vr2", "OT'", "vr3", "AT0",
             "red",
             "attT", "AT1", "wo", "x2T",
             "kkrr", "ffn"]
SECTIONS = {
    "prologue": list(L0_USES),
    "first": [u for u in STEP_USES if not u.endswith("'")],
    "loop": list(STEP_USES),
    "last": [u for u in STEP_USES if u not in L0_USES],
    "tail": ["AT2'", "AT3'", "Y'", "OT'"],
}
LOOP_STEPS = B - 2
SETUP_STEPS = 12


def scratch_plan():
    plan, total, of_bank = {}, 0, [0, 0]
    for section, uses in SECTIONS.items():
        times = LOOP_STEPS if section == "loop" else 1
        steps = (len(uses), [len(uses[n::2]) for n in range(2)])
        for n, name in enumerate(uses):
            bank = n % 2
            plan[section, name] = (bank, total + n, of_bank[bank] + n // 2,
                                   steps[0] if section == "loop" else 0,
                                   steps[1][bank] if section == "loop" else 0)
        total += times * steps[0]
        of_bank = [of_bank[n] + times * steps[1][n] for n in range(2)]
    return plan


def rwkv_then_attention(nc, x, ctx_in, consts, state0, l0w, maa_w1, maa_w2, decay_w1, decay_w2,
                        wqkv, winj, wo1, bo, out):
    plan = scratch_plan()
    with ExitStack() as stack:
        def sb(name, shape, dt=F32):
            return stack.enter_context(nc.sbuf_tensor(name, shape, dt))

        def psum(name, shape, dt=F32):
            return stack.enter_context(nc.psum_tensor(name, shape, dt))

        def sem(name):
            return stack.enter_context(nc.semaphore(name))

        cst = sb("cst", [P, NCONST])
        s0_all = sb("s0_all", [P, B, ET, SD])
        l0w_sb = sb("l0w_sb", [P, len(L0W), ET, E])
        w1_sb = sb("w1_sb", [P, ET, MIX * XM])
        w2a_sb = sb("w2a_sb", [P, 4, E])
        w2b_sb = sb("w2b_sb", [XM, E])
        dw1_sb = sb("dw1_sb", [P, ET, XD])
        dw2_sb = sb("dw2_sb", [XD, E])
        wqkv_sb = sb("wqkv_sb", [P, 2, 3 * HD])
        winj_sb = sb("winj_sb", [P, 2, 3 * HD])
        wo1_sb = sb("wo1_sb", [P, NP, P])
        bo_sb = sb("bo_sb", [1, P])
        ident = sb("ident", [P, P])
        head_ones = sb("head_ones", [P, HT])
        ones_row = sb("ones_row", [1, P])
        minus_half = sb("minus_half", [P, H0])
        one = sb("one", [P, 1])
        eps_row = sb("eps_row", [P, ET])
        carrier = sb("carrier", [P, 2])
        q_bias = sb("q_bias", [P, NP])

        x_sb = sb("x_sb", [P, E])
        st1 = sb("st1", [P, 6])
        mv1 = sb("mv1", [P, 2])
        ve1 = sb("ve1", [P, 1])
        rstd1 = sb("rstd1", [P, 1])
        xhat = sb("xhat", [P, E])
        xn = sb("xn", [P, ET, T + 1])
        sx = sb("sx", [P, ET, T])
        xin = sb("xin", [P, ET, T])
        xxx = sb("xxx", [P, T])
        xxx4 = sb("xxx4", [XM, T])
        x5 = sb("x5", [P, MIX, ET, T])
        dtanh = sb("dtanh", [XD, T])
        dexp = sb("dexp", [P, ET, T])
        w_sb = sb("w_sb", [P, ET, T])
        kr_sb = sb("kr_sb", [P, 2, ET, T])
        bonus = sb("bonus", [P, ET, T])
        v_sb = sb("v_sb", [P, E])
        vrep = sb("vrep", [P, 4, 4, P])
        g_sb = sb("g_sb", [P, ET, T])
        g_tanh = sb("g_tanh", [P, ET, T])
        gate = sb("gate", [P, ET, T])
        kv = sb("kv", [P, ET, SD, T])
        states = sb("states", [P, ET, SD, T + 1])
        bonus_v = sb("bonus_v", [P, E])
        att = sb("att", [P, E])
        hsum = sb("hsum", [P, H0])
        cent = sb("cent", [P, E])
        sq = sb("sq", [P, E])
        hsq = sb("hsq", [P, H0])
        hve = sb("hve", [P, H0])
        hrstd = sb("hrstd", [P, H0])
        yhat = sb("yhat", [P, E])
        yT = sb("yT", [P, ET, T])
        ygT = sb("ygT", [P, ET, T])
        x1 = sb("x1", [P, E])
        st2 = sb("st2", [P, 6])
        mv2 = sb("mv2", [P, 2])
        ve2 = sb("ve2", [P, 1])
        rstd2 = sb("rstd2", [P, 1])
        xhat2 = sb("xhat2", [P, E])
        xn2 = sb("xn2", [P, ET, T + 1])
        sx2 = sb("sx2", [P, ET, T])
        xk = sb("xk", [P, ET, T])
        xr = sb("xr", [P, ET, T])
        krelu = sb("krelu", [P, ET, T])
        ksq = sb("ksq", [P, ET, T])
        rtanh = sb("rtanh", [P, E])
        rsig = sb("rsig", [P, E])
        ffn_r = sb("ffn_r", [P, E])

        z_sb = sb("z_sb", [P, E])
        zres = sb("zres", [P, E])
        u_in = sb("u_in", [P, E])
        u_sb = sb("u_sb", [P, E])
        q_sb = sb("q_sb", [P, 2, E])
        k_sb = sb("k_sb", [P, 2, E])
        v1_sb = sb("v1_sb", [P, ET, NH, VW])
        nmax = sb("nmax", [P, 2, 2, ET])
        prob = sb("prob", [P, 2, 2, ET, E])
        probT = sb("probT", [P, 2, 2, ET, ET, P])
        rden = sb("rden", [P, 2, ET, 1])
        attn = sb("attn", [P, ET, HD])
        attnT = sb("attnT", [P, NP, E])
        st3 = sb("st3", [P, ET, 6])
        mv3 = sb("mv3", [P, ET, 2])
        ve3 = sb("ve3", [P, ET])
        rstd3 = sb("rstd3", [P, ET])
        yn = sb("yn", [P, ET, P])
        o_sb = sb("o_sb", [P, E])

        qk_ps = psum("qk_ps", [P, 2, E])
        s_ps = [psum(f"s_ps{h}", [P, ET, E]) for h in range(2)]
        t_ps = [psum(f"t_ps{h}", [P, ET, ET, P]) for h in range(2)]
        o_ps = psum("o_ps", [P, 2, ET, P])
        scr = [psum(f"scr{n}", [P, 512]) for n in range(2)]

        x_in, u_loaded, out_stored = sem("x_in"), sem("u_loaded"), sem("out_stored")
        in_cst, in_l0a, in_l0b, in_l1a, in_l1b = (sem(f"in_{n}") for n in ("cst", "l0a", "l0b", "l1a", "l1b"))
        setup = sem("setup")
        bias_scaled = sem("bias_scaled")
        scr_ready = sem("scr_ready")
        scr_free = [sem(f"scr_free{n}") for n in range(2)]
        stats1, mean1, eps1, rstd1_s, xhat_s = (sem(n) for n in ("stats1", "mean1", "eps1", "rstd1_s", "xhat_s"))
        prev1_s, sx_s, xin_s = (sem(n) for n in ("prev1_s", "sx_s", "xin_s"))
        x5_s = sem("x5_s")
        w_s, bonus_s, gate_s = sem("w_s"), sem("bonus_s"), sem("gate_s")
        s0_s = sem("s0_s")
        vrep_s = sem("vrep_s")
        scan_s = sem("scan_s")
        rs_s = sem("rs_s")
        gn_s = sem("gn_s")
        hrstd_s, yhat_s, ygT_s = (sem(n) for n in ("hrstd_s", "yhat_s", "ygT_s"))
        stats2, mean2, eps2, rstd2_s, xhat2_s = (sem(n) for n in ("stats2", "mean2", "eps2", "rstd2_s", "xhat2_s"))
        prev2_s, sx2_s, xkr_s = (sem(n) for n in ("prev2_s", "sx2_s", "xkr_s"))
        ksq_s, rsig_s, ffnr_s, z_s, zres_s, u_s = (sem(n) for n in ("ksq_s", "rsig_s", "ffnr_s", "z_s", "zres_s", "u_s"))
        proj_s = sem("proj_s")
        qk_s = sem("qk_s")
        score_s = sem("score_s")
        max_s = sem("max_s")
        prob_s = sem("prob_s")
        turn_s = sem("turn_s")
        probT_s = [sem("probT_s0"), sem("probT_s1")]
        pv_s = sem("pv_s")
        rden_s = sem("rden_s")
        attn_s = sem("attn_s")
        stats3, mean3, eps3, rstd3_s, yn_s = (sem(n) for n in ("stats3", "mean3", "eps3", "rstd3_s", "yn_s"))

        block = stack.enter_context(nc.Block())

        def col(name, n=0):
            return cst[:, COL[name] + n:COL[name] + n + 1]

        def l0_weight(name):
            return l0w_sb[:, L0W.index(name), :, :]

        def use(section, name, b):
            bank, before, bank_before, step, bank_step = plan[section, name]
            if section != "loop":
                return bank, before + 1, bank_before
            return bank, (b - 1) * step + (before + 1), (b - 1) * bank_step + bank_before

        def run_steps(eng, step, tail=None):
            step("first", 0)
            with eng.Fori(1, B - 1) as b:
                step("loop", b)
            step("last", B - 1)
            if tail:
                tail()

        @block.sync
        def _(sp):
            sp.dma_start(x_sb[:, :], x[0]).then_inc(x_in, 16)
            sp.dma_start(cst[:, :], consts).then_inc(in_cst, 16)
            sp.dma_start(w1_sb[:, :, :], maa_w1).then_inc(in_l0a, 16)
            sp.wait_ge(setup, 1)
            for m in range(4):
                rows = slice(m * XM, (m + 1) * XM)
                sp.dma_start(w2a_sb[rows, m, :], maa_w2[rows, :]).then_inc(in_l0a, 16)
            sp.dma_start(w2b_sb[:, :], maa_w2[4 * XM:5 * XM, :]).then_inc(in_l0a, 16)
            sp.dma_start(dw1_sb[:, :, :], decay_w1).then_inc(in_l0a, 16)
            sp.dma_start(dw2_sb[:, :], decay_w2).then_inc(in_l0a, 16)
            sp.dma_start(s0_all[:, :, :, :], state0).then_inc(in_cst, 16)
            sp.dma_start(l0w_sb[:, 0:4, :, :], l0w[:, 0:4]).then_inc(in_l0a, 16)
            sp.dma_start(l0w_sb[:, 4:8, :, :], l0w[:, 4:8]).then_inc(in_l0b, 16)
            sp.dma_start(u_in[:, :], ctx_in[0]).then_inc(u_loaded, 16)
            sp.dma_start(wqkv_sb[:, :, :], wqkv).then_inc(in_l1a, 16)
            sp.dma_start(winj_sb[:, :, :], winj).then_inc(in_l1a, 16)
            sp.dma_start(wo1_sb[:, :, :], wo1).then_inc(in_l1b, 16)
            sp.dma_start(bo_sb[:, :], bo).then_inc(in_l1b, 16)

            def load_next(section, b):
                bank, _, before = use(section, "wo", b - 1)
                sp.wait_ge(scr_free[bank], before + 1)
                sp.dma_start(x_sb[:, :], x[b + 1]).then_inc(x_in, 16)
                sp.wait_ge(u_s, b + 1)
                sp.dma_start(u_in[:, :], ctx_in[b + 1]).then_inc(u_loaded, 16)

            def store(section, b):
                bank, _, before = use(section, "OT'", b + 1)
                sp.wait_ge(scr_free[bank], before + 1)
                sp.dma_start(out[b], o_sb[:, :]).then_inc(out_stored, 16)

            load_next("prologue", 0)
            load_next("first", 1)
            with sp.Fori(1, B - 2) as b:
                store("loop", b - 1)
                load_next("loop", b + 1)
            store("loop", B - 3)
            store("last", B - 2)
            store("tail", B - 1)
            sp.wait_ge(out_stored, 16 * B)

        @block.gpsimd
        def _(pool):
            done = 0

            def chained(ins):
                nonlocal done
                done += 1
                ins.then_inc(setup, 1)
                pool.wait_ge(setup, done)

            chained(pool.memset(w2a_sb[:, :, :], 0.0))
            chained(pool.memset(ident[:, :], 0.0))
            chained(pool.affine_select(out=ident[:, :], in_=ident[:, :], compare_op=ALU.not_equal, fill=1.0,
                                       base=0, pattern=[[-1, P]], channel_multiplier=1))
            chained(pool.memset(head_ones[:, :], 1.0))
            chained(pool.affine_select(out=head_ones[:, :], in_=head_ones[:, :], compare_op=ALU.is_ge, fill=0.0,
                                       base=0, pattern=[[-SD, HT]], channel_multiplier=1))
            chained(pool.affine_select(out=head_ones[:, :], in_=head_ones[:, :], compare_op=ALU.is_ge, fill=0.0,
                                       base=SD - 1, pattern=[[SD, HT]], channel_multiplier=-1))
            chained(pool.memset(minus_half[:, :], -0.5))
            chained(pool.memset(ones_row[:, :], 1.0))
            chained(pool.memset(one[:, :], 1.0))
            chained(pool.memset(eps_row[:, :], EPS))
            chained(pool.memset(carrier[:, :], 0.0))
            chained(pool.memset(v1_sb[:, :, :, DH:VW], 1.0))
            pool.wait_ge(in_cst, 32)
            pool.tensor_scalar(q_bias[:, :], cst[:, COL["q_bias"]:COL["q_bias"] + NP], SCALE, None,
                               ALU.mult).then_inc(bias_scaled, 1)

            def copy(dst, src, shape):
                ones = one[:, :]
                while len(ones.shape) < len(shape):
                    ones = ones[:, None]
                return pool.tensor_tensor(dst, src, ones.to_broadcast(shape), ALU.mult)

            def rsqrt(var, ve, rstd, n, wait_var, eps_sem, rstd_sem, val):
                pool.wait_ge(wait_var, val)
                pool.tensor_tensor(ve, var, eps_row[:, 0:n], ALU.add).then_inc(eps_sem, 1)
                pool.wait_ge(eps_sem, val)
                pool.tensor_tensor(rstd, ve, minus_half[:, 0:n], ALU.pow).then_inc(rstd_sem, 1)

            def shifted_rows(c):
                n = COL["prev"]
                prev = cst[:, n:n + 2 * B * ET].rearrange("p (r b t) -> p r b t", r=2, b=B)
                pool.tensor_copy(xn[:, :, 0:1], prev[:, 0, bass.ds(c, 1), :].rearrange("p b t -> p t b")).then_inc(prev1_s, 1)
                pool.tensor_copy(xn2[:, :, 0:1], prev[:, 1, bass.ds(c, 1), :].rearrange("p b t -> p t b")).then_inc(prev2_s, 1)

            def first_states(c):
                pool.tensor_copy(states[:, :, :, 0:1],
                                 s0_all[:, bass.ds(c, 1), :, :].rearrange("p b t d -> p t d b")).then_inc(s0_s, 1)

            def mix_add(section, c, n):
                name, slots = MIX_USES[n]
                bank, _, before = use(section, name, c - 1)
                pool.wait_ge(scr_free[bank], before + 1)
                a, z = slots[0], slots[-1] + 1
                xb = xn[:, None, :, 1:T + 1].to_broadcast([P, z - a, ET, T])
                pool.tensor_tensor(x5[:, a:z, :, :], x5[:, a:z, :, :], xb, ALU.add).then_inc(x5_s, 1)

            def spread_v(section, c):
                bank, _, before = use(section, "vg", c - 1)
                pool.wait_ge(scr_free[bank], before + 1)
                for n in range(4):
                    t, dh = n // 2, n % 2
                    src = v_sb[:, t * P:(t + 1) * P].rearrange("p (h d) -> p d h", d=SD)[:, dh * 4:dh * 4 + 4, :]
                    dst = vrep[:, n, :, :].rearrange("p d (h k) -> p d h k", k=SD)
                    src = src[:, :, :, None].to_broadcast([P, 4, HT, SD])
                    if n == 0:
                        last = copy(dst, src, [P, 4, HT, SD])
                    else:
                        last = pool.tensor_copy(dst, src)
                    last.then_inc(vrep_s, 1)

            def receive(c, n):
                t, dh = n // 2, n % 2
                d = slice(dh * 4, dh * 4 + 4)
                pool.wait_ge(scan_s, 4 * c + n + 1)
                r = kr_sb[:, 1, t:t + 1, :].to_broadcast([P, 4, T])
                pool.tensor_tensor(kv[:, t, d, :], states[:, t, d, 0:T], r, ALU.mult).then_inc(rs_s, 1)

            def l0(section, c, slot):
                if slot == 0:
                    rsqrt(mv1[:, 1:2], ve1[:, :], rstd1[:, :], 1, mean1, eps1, rstd1_s, c + 1)
                    shifted_rows(c)
                    mix_add(section, c, 0)
                if slot == 1:
                    mix_add(section, c, 1)
                    mix_add(section, c, 2)
                if slot == 3:
                    spread_v(section, c)
                    first_states(c)
                if slot == 5:
                    for n in range(4):
                        receive(c, n)
                    pool.wait_ge(gn_s, 7 * c + 7)
                    pool.tensor_tensor(hrstd[:, :], hve[:, :], minus_half[:, :], ALU.pow).then_inc(hrstd_s, 1)
                if slot == 6:
                    rsqrt(mv2[:, 1:2], ve2[:, :], rstd2[:, :], 1, mean2, eps2, rstd2_s, c + 1)

            def finish(b):
                rsqrt(mv3[:, :, 1], ve3[:, :], rstd3[:, :], ET, mean3, eps3, rstd3_s, b + 1)

            def keep_z(section, b):
                if section != "first":
                    pool.wait_ge(scr_ready, use(section, "Y'", b)[1])
                pool.wait_ge(z_s, b + 1)
                copy(zres[:, :], z_sb[:, :], [P, E]).then_inc(zres_s, 1)

            def take_u(b):
                pool.wait_ge(proj_s, NP * b)
                pool.wait_ge(u_loaded, 16 * (b + 1))
                copy(u_sb[:, :], u_in[:, :], [P, E]).then_inc(u_s, 1)

            def step(section, b):
                for slot in range(NP):
                    if section != "last":
                        l0(section, b + 1, slot)
                    if slot == 4:
                        if section != "first":
                            finish(b - 1)
                        keep_z(section, b)
                if section != "last":
                    take_u(b + 1)

            pool.wait_ge(u_loaded, 16)
            pool.tensor_copy(u_sb[:, :], u_in[:, :]).then_inc(u_s, 1)
            for slot in range(NP):
                l0("prologue", 0, slot)
            run_steps(pool, step, lambda: finish(B - 1))

        @block.scalar
        def _(act):
            def l0_scratch(section, c, name):
                bank, ready, _ = use(section, name, c - 1)
                act.wait_ge(scr_ready, ready)
                return scr[bank], scr_free[bank]

            def mix_tanh(section, c):
                ps, free = l0_scratch(section, c, "mixin")
                act.activation(xxx[:, :], ps[:, 0:T], ACT.Tanh)
                act.activation(xxx4[:, :], ps[0:XM, T:2 * T], ACT.Tanh).then_inc(free, 1)

            def decay_tanh(section, c):
                ps, free = l0_scratch(section, c, "dec1")
                act.activation(dtanh[:, :], ps[0:XD, 0:T], ACT.Tanh).then_inc(free, 1)

            def decay_exp(section, c):
                ps, free = l0_scratch(section, c, "dec2")
                for t in range(ET):
                    last = act.activation(dexp[:, t, :], ps[:, t * T:(t + 1) * T], ACT.Exp, bias=col("decay", t))
                last.then_inc(free, 1)
                _, _, before = use(section, "dec2", c - 1)
                act.wait_ge(free, before + 1)
                act.activation(w_sb[:, :, :], dexp[:, :, :], ACT.Exp, scale=-1.0).then_inc(w_s, 1)

            def key_receptance(section, c):
                ps, free = l0_scratch(section, c, "kr")
                act.activation(kr_sb[:, :, :, :], ps[:, :].rearrange("p (a t n) -> p a t n", a=2, t=ET),
                               ACT.Copy).then_inc(free, 1)

            def value_gate(section, c):
                ps, free = l0_scratch(section, c, "vg")
                g = ps[:, E:2 * E].rearrange("p (t n) -> p t n", t=ET)
                act.activation(v_sb[:, :], ps[:, 0:E], ACT.Copy)
                act.activation(g_sb[:, :, :], g, ACT.Copy)
                act.activation(g_tanh[:, :, :], g, ACT.Tanh, scale=0.5).then_inc(free, 1)

            def norm_affine(section, c):
                ps, free = l0_scratch(section, c, "attT")
                for t in range(ET):
                    last = act.activation(yT[:, t, :], ps[:, t * T:(t + 1) * T], ACT.Identity,
                                          scale=col("gn_w", t), bias=col("gn_b", t))
                last.then_inc(free, 1)

            def ffn_act(section, c):
                ps, free = l0_scratch(section, c, "kkrr")
                act.activation(krelu[:, :, :], ps[:, 0:E].rearrange("p (t n) -> p t n", t=ET),
                               ACT.Relu)
                act.activation(rtanh[:, :], ps[:, E:2 * E], ACT.Tanh, scale=0.5).then_inc(free, 1)

            def exps(g, p, h):
                par = p % 2
                act.wait_ge(max_s, 16 * g + 2 * p + h + 1)
                for it in range(ET):
                    last = act.activation(prob[:, par, h, it, :], s_ps[h][:, it, :], ACT.Exp,
                                          bias=nmax[:, par, h, it:it + 1])
                last.then_inc(prob_s, 1)

            def turned(b, p):
                act.wait_ge(turn_s, 16 * b + 2 * p + 2)
                act.activation(probT[:, p % 2, 1, :, :, :], t_ps[1][:, :, :, :], ACT.Copy).then_inc(probT_s[1], 1)

            def values(section, b, name):
                bank, ready, _ = use(section, name, b)
                act.wait_ge(scr_ready, ready)
                oh, lt = int(name[1]), int(name[2])
                act.activation(v1_sb[:, lt, 8 * oh:8 * oh + 8, 0:DH],
                               scr[bank][:, :].rearrange("p (h d) -> p h d", h=8), ACT.Copy).then_inc(scr_free[bank], 1)

            def l0(section, c, slot, phase):
                if (slot, phase) == (0, "b"):
                    mix_tanh(section, c)
                if (slot, phase) == (2, "a"):
                    decay_tanh(section, c)
                if (slot, phase) == (2, "b"):
                    decay_exp(section, c)
                if (slot, phase) == (2, "c"):
                    key_receptance(section, c)
                if (slot, phase) == (3, "a"):
                    value_gate(section, c)
                if (slot, phase) == (6, "a"):
                    norm_affine(section, c)
                if (slot, phase) == (7, "a"):
                    ffn_act(section, c)

            def step(section, b):
                for p in range(NP):
                    exps(b, p, 0)
                    exps(b, p, 1)
                    if section != "last":
                        l0(section, b + 1, p, "a")
                    if p > 0:
                        turned(b, p - 1)
                    elif section != "first":
                        turned(b - 1, NP - 1)
                    if section != "last":
                        l0(section, b + 1, p, "b")
                    if p == 3:
                        values(section, b, "V10")
                        values(section, b, "V11")
                    if p == 1:
                        values(section, b, "V00")
                        values(section, b, "V01")
                    if section != "last":
                        l0(section, b + 1, p, "c")

            act.wait_ge(in_cst, 32)
            for slot in range(NP):
                for phase in "abc":
                    l0("prologue", 0, slot, phase)
            run_steps(act, step, lambda: turned(B - 1, NP - 1))

        @block.vector
        def _(dve):
            def wait_apart(s, val):
                dve.wait_ge(s, val)
                dve.tensor_copy(carrier[:, 1:2], carrier[:, 0:1])

            def scratch(section, b, name):
                bank, ready, _ = use(section, name, b)
                dve.wait_ge(scr_ready, ready)
                return scr[bank], scr_free[bank]

            def layer_stats(src, wait, val, st, mv, st_sem, mv_sem, n):
                dve.wait_ge(wait, val)
                dve.bn_stats(st, src).then_inc(st_sem, 1)
                wait_apart(st_sem, n)
                dve.bn_aggr(mv, st).then_inc(mv_sem, 1)

            def normalise(dst, src, mv, rstd, wait, n, ready):
                dve.wait_ge(wait, n)
                dve.tensor_scalar(dst, src, mv[:, 0:1], rstd[:, 0:1], ALU.subtract, ALU.mult).then_inc(ready, 1)

            def shift_in(section, c, name, dst, ln, prev, diff, diff_sem):
                ps, free = scratch(section, c - 1, name)
                for t in range(ET):
                    last = dve.tensor_scalar(dst[:, t, 1:T + 1], ps[:, t * T:(t + 1) * T],
                                             col(ln + "_w", t), col(ln + "_b", t), ALU.mult, ALU.add)
                last.then_inc(free, 1)
                dve.wait_ge(prev, c + 1)
                dve.wait_ge(free, use(section, name, c - 1)[2] + 1)
                dve.tensor_tensor(diff[:, :, :], dst[:, :, 0:T], dst[:, :, 1:T + 1], ALU.subtract).then_inc(diff_sem, 1)
                dve.wait_ge(diff_sem, c + 1)

            def mix_in(c):
                for t in range(ET):
                    last = dve.scalar_tensor_tensor(xin[:, t, :], sx[:, t, :], col("maa_x", t), xn[:, t, 1:T + 1],
                                                    ALU.mult, ALU.add)
                last.then_inc(xin_s, 1)

            def mixes(section, c, n):
                name, slots = MIX_USES[n]
                ps, free = scratch(section, c - 1, name)
                for k, slot in enumerate(slots):
                    for t in range(ET):
                        last = dve.scalar_tensor_tensor(
                            x5[:, slot, t, :], ps[:, (k * ET + t) * T:(k * ET + t + 1) * T],
                            col("maa", MIX_ORDER[slot] * ET + t), sx[:, t, :], ALU.add, ALU.mult)
                last.then_inc(free, 1)

            def bonus_rk(section, c):
                bank, _, before = use(section, "kr", c - 1)
                dve.wait_ge(scr_free[bank], before + 1)
                for t in range(ET):
                    last = dve.scalar_tensor_tensor(bonus[:, t, :], kr_sb[:, 1, t, :], col("bonus", t),
                                                    kr_sb[:, 0, t, :], ALU.mult, ALU.mult)
                last.then_inc(bonus_s, 1)

            def make_gate(section, c):
                bank, _, before = use(section, "vg", c - 1)
                dve.wait_ge(scr_free[bank], before + 1)
                dve.scalar_tensor_tensor(gate[:, :, :], g_tanh[:, :, :], 1.0, g_sb[:, :, :],
                                         ALU.add, ALU.mult).then_inc(gate_s, 1)

            def key_value(section, c, n):
                t, dh = n // 2, n % 2
                ps, free = scratch(section, c - 1, f"vr{n}")
                k = kr_sb[:, 0, t:t + 1, :].to_broadcast([P, 4, T])
                dve.tensor_tensor(kv[:, t, dh * 4:dh * 4 + 4, :], ps[:, :].rearrange("p (d n) -> p d n", d=4), k,
                                  ALU.mult).then_inc(free, 1)

            def scans(section, c, n):
                t, dh = n // 2, n % 2
                bank, _, before = use(section, f"vr{n}", c - 1)
                dve.wait_ge(scr_free[bank], before + 1)
                if n == 0:
                    dve.wait_ge(w_s, c + 1)
                    dve.wait_ge(s0_s, c + 1)
                for d in range(dh * 4, dh * 4 + 4):
                    last = dve.tensor_tensor_scan(states[:, t, d, 1:T + 1], w_sb[:, t, :], kv[:, t, d, :],
                                                  states[:, t, d, 0:1], ALU.mult, ALU.add)
                last.then_inc(scan_s, 1)

            def group_norm(section, c):
                ps, free = scratch(section, c - 1, "red")
                n = 7 * c

                def heads(a):
                    return a.rearrange("p (h d) -> p h d", d=SD)

                def spread(a):
                    return a.rearrange("p (h o) -> p h o", o=1).to_broadcast([P, H0, SD])

                dve.tensor_tensor(heads(bonus_v[:, :]), heads(v_sb[:, :]), spread(ps[:, E:E + H0]), ALU.mult).then_inc(gn_s, 1)
                dve.wait_ge(gn_s, n + 1)
                dve.tensor_tensor(att[:, :], ps[:, 0:E], bonus_v[:, :], ALU.add).then_inc(free, 1)
                dve.wait_ge(free, use(section, "red", c - 1)[2] + 1)
                dve.tensor_reduce(hsum[:, :], heads(att[:, :]), AX.X, ALU.add).then_inc(gn_s, 1)
                dve.wait_ge(gn_s, n + 2)
                dve.scalar_tensor_tensor(heads(cent[:, :]), spread(hsum[:, :]), -1.0 / SD, heads(att[:, :]),
                                         ALU.mult, ALU.add).then_inc(gn_s, 1)
                dve.wait_ge(gn_s, n + 3)
                dve.tensor_tensor(sq[:, :], cent[:, :], cent[:, :], ALU.mult).then_inc(gn_s, 1)
                dve.wait_ge(gn_s, n + 4)
                dve.tensor_reduce(hsq[:, :], heads(sq[:, :]), AX.X, ALU.add).then_inc(gn_s, 1)
                dve.wait_ge(gn_s, n + 5)
                dve.tensor_scalar(hve[:, :], hsq[:, :], 1.0 / SD, EPS, ALU.mult, ALU.add).then_inc(gn_s, 2)
                dve.wait_ge(hrstd_s, c + 1)
                dve.tensor_tensor(heads(yhat[:, :]), heads(cent[:, :]), spread(hrstd[:, :]), ALU.mult).then_inc(yhat_s, 1)

            def gated(section, c):
                bank, _, before = use(section, "attT", c - 1)
                dve.wait_ge(scr_free[bank], before + 1)
                dve.scalar_tensor_tensor(ygT[:, :, :], gate[:, :, :], 0.5, yT[:, :, :], ALU.mult,
                                         ALU.mult).then_inc(ygT_s, 1)

            def residual1(section, c):
                ps, free = scratch(section, c - 1, "wo")
                dve.tensor_tensor(x1[:, :], ps[:, 0:E], x_sb[:, :], ALU.add).then_inc(free, 1)
                layer_stats(x1[:, :], free, use(section, "wo", c - 1)[2] + 1, st2[:, :], mv2[:, :], stats2, mean2, c + 1)
                normalise(xhat2[:, :], x1[:, :], mv2, rstd2, rstd2_s, c + 1, xhat2_s)

            def ffn_in(section, c):
                shift_in(section, c, "x2T", xn2, "ln2", prev2_s, sx2, sx2_s)
                for dst, name in ((xk, "ffn_k"), (xr, "ffn_r")):
                    for t in range(ET):
                        last = dve.scalar_tensor_tensor(dst[:, t, :], sx2[:, t, :], col(name, t),
                                                        xn2[:, t, 1:T + 1], ALU.mult, ALU.add)
                last.then_inc(xkr_s, 1)

            def ffn_mid(section, c):
                bank, _, before = use(section, "kkrr", c - 1)
                dve.wait_ge(scr_free[bank], before + 1)
                dve.tensor_tensor(ksq[:, :, :], krelu[:, :, :], krelu[:, :, :], ALU.mult).then_inc(ksq_s, 1)
                dve.tensor_scalar(rsig[:, :], rtanh[:, :], 0.5, 0.5, ALU.mult, ALU.add).then_inc(rsig_s, 1)

            def make_z(section, c):
                ps, free = scratch(section, c - 1, "ffn")
                dve.wait_ge(rsig_s, c + 1)
                dve.tensor_tensor(ffn_r[:, :], ps[:, 0:E], rsig[:, :], ALU.mult).then_inc(free, 1)
                dve.wait_ge(free, use(section, "ffn", c - 1)[2] + 1)
                if section != "prologue":
                    dve.wait_ge(proj_s, NP * c)
                    dve.wait_ge(zres_s, c)
                dve.tensor_tensor(z_sb[:, :], ffn_r[:, :], x1[:, :], ALU.add).then_inc(z_s, 1)

            def qk_out(g, p):
                par = p % 2
                dve.wait_ge(proj_s, NP * g + p + 1)
                dve.tensor_scalar(q_sb[:, par, :], qk_ps[:, 0, :], SCALE, q_bias[:, p:p + 1], ALU.mult,
                                  ALU.add).then_inc(qk_s, 1)
                dve.tensor_copy(k_sb[:, par, :], qk_ps[:, 1, :]).then_inc(qk_s, 1)

            def maxes(b, p, h):
                dve.wait_ge(score_s, 16 * b + 2 * p + h + 1)
                dve.tensor_reduce(nmax[:, p % 2, h, :], s_ps[h][:, :, :], AX.X, ALU.max, negate=True).then_inc(max_s, 1)

            def turned(b, p):
                dve.wait_ge(turn_s, 16 * b + 2 * p + 1)
                dve.tensor_copy(probT[:, p % 2, 0, :, :, :], t_ps[0][:, :, :, :]).then_inc(probT_s[0], 1)

            def attended(b, p):
                dve.wait_ge(pv_s, NP * b + p + 1)
                dve.reciprocal(rden[:, :, :, :], o_ps[:, :, :, DH:VW]).then_inc(rden_s, 1)
                dve.wait_ge(rden_s, NP * b + p + 1)
                dst = attn[:, :, 2 * p * DH:2 * (p + 1) * DH].rearrange("p i (h d) -> p h i d", h=2)
                dve.tensor_tensor(dst, o_ps[:, :, :, 0:DH], rden[:, :, :, :].to_broadcast([P, 2, ET, DH]),
                                  ALU.mult).then_inc(attn_s, 1)

            def attention_turned(section, b, name):
                ps, free = scratch(section, b, name)
                k = int(name[2])
                dve.tensor_copy(attnT[:, 2 * k:2 * k + 2, :], ps[:, :].rearrange("p (a n) -> p a n", a=2)).then_inc(free, 1)

            def finish(section, b):
                ps, free = scratch(section, b, "Y'")
                y = ps[:, 0:E].rearrange("p (t n) -> p t n", t=ET)
                for t in range(ET):
                    last = dve.bn_stats(st3[:, t, :], y[:, t, :])
                    last.then_inc(stats3, 1)
                wait_apart(stats3, 2 * b)
                for t in range(ET):
                    last = dve.bn_aggr(mv3[:, t, :], st3[:, t, :])
                last.then_inc(mean3, 1)
                dve.wait_ge(rstd3_s, b)
                for t in range(ET):
                    last = dve.tensor_scalar(yn[:, t, :], y[:, t, :], mv3[:, t, 0:1], rstd3[:, t:t + 1],
                                             ALU.subtract, ALU.mult)
                    last.then_inc(free if t else yn_s, 1)

            def store_out(section, b):
                ps, free = scratch(section, b, "OT'")
                if section == "tail":
                    dve.wait_ge(out_stored, 16 * (b - 1))
                dve.tensor_copy(o_sb[:, :], ps[:, 0:E]).then_inc(free, 1)

            def l0(section, c, slot, phase):
                at = (slot, phase)
                if at == (0, "a"):
                    layer_stats(x_sb[:, :], x_in, 16 * (c + 1), st1[:, :], mv1[:, :], stats1, mean1, c + 1)
                    normalise(xhat[:, :], x_sb[:, :], mv1, rstd1, rstd1_s, c + 1, xhat_s)
                    shift_in(section, c, "xT", xn, "ln1", prev1_s, sx, sx_s)
                    mix_in(c)
                if at == (0, "c"):
                    mixes(section, c, 0)
                if at == (1, "a"):
                    mixes(section, c, 1)
                if at == (1, "b"):
                    mixes(section, c, 2)
                if at == (3, "a"):
                    bonus_rk(section, c)
                    make_gate(section, c)
                if at == (3, "b"):
                    key_value(section, c, 0)
                if at == (3, "c"):
                    key_value(section, c, 1)
                    scans(section, c, 0)
                if at == (4, "a"):
                    key_value(section, c, 2)
                    scans(section, c, 1)
                if at == (4, "b"):
                    key_value(section, c, 3)
                    scans(section, c, 2)
                if at == (4, "c"):
                    scans(section, c, 3)
                if at == (5, "c"):
                    group_norm(section, c)
                if at == (6, "a"):
                    gated(section, c)
                if at == (6, "b"):
                    residual1(section, c)
                if at == (6, "c"):
                    ffn_in(section, c)
                if at == (7, "a"):
                    ffn_mid(section, c)
                if at == (7, "b"):
                    make_z(section, c)

            def left_over(section, b, slot, phase):
                at = (slot, phase)
                if at == (0, "c"):
                    attention_turned(section, b, "AT2'")
                if at == (2, "a"):
                    attention_turned(section, b, "AT3'")
                if at == (3, "a"):
                    finish(section, b)
                if at == (4, "a"):
                    store_out(section, b)

            def step(section, b):
                for p in range(NP):
                    maxes(b, p, 0)
                    maxes(b, p, 1)
                    if section != "last":
                        l0(section, b + 1, p, "a")
                    if section != "first":
                        left_over(section, b, p, "a")
                    if p < NP - 1:
                        qk_out(b, p + 1)
                    if p > 0:
                        turned(b, p - 1)
                    elif section != "first":
                        turned(b - 1, NP - 1)
                    if p == 6:
                        attention_turned(section, b, "AT1")
                    if section != "last":
                        l0(section, b + 1, p, "b")
                    if p > 1:
                        attended(b, p - 2)
                    elif section != "first":
                        attended(b - 1, NP - 2 + p)
                    if section != "last":
                        l0(section, b + 1, p, "c")
                    if section != "first":
                        left_over(section, b, p, "c")
                    if p == 4:
                        attention_turned(section, b, "AT0")
                if section == "loop":
                    dve.wait_ge(out_stored, 16 * b)
                if section != "last":
                    qk_out(b + 1, 0)

            def tail():
                turned(B - 1, NP - 1)
                attended(B - 1, NP - 2)
                attention_turned("tail", B, "AT2'")
                attended(B - 1, NP - 1)
                attention_turned("tail", B, "AT3'")
                finish("tail", B)
                store_out("tail", B)

            dve.wait_ge(in_cst, 32)
            dve.wait_ge(setup, SETUP_STEPS)
            dve.wait_ge(bias_scaled, 1)
            for slot in range(NP):
                for phase in "abc":
                    l0("prologue", 0, slot, phase)
            qk_out(0, 0)
            run_steps(dve, step, tail)

        @block.tensor
        def _(pe):
            def read(section, b, name):
                bank, _, before = use(section, name, b)
                pe.wait_ge(scr_free[bank], before + 1)

            def scratch(section, b, name):
                bank, _, before = use(section, name, b)
                if section != "prologue" or before > 0:
                    pe.wait_ge(scr_free[bank], before)
                return scr[bank]

            def tokens_first(ps, weight, src, col0=0):
                for t in range(ET):
                    last = pe.matmul(ps[:, col0:col0 + E], src[:, t, :], weight[:, t, :], start=(t == 0), stop=(t == ET - 1))
                return last

            def channels_first(ps, weight, src, col0=0):
                for f in range(ET):
                    for t in range(ET):
                        last = pe.matmul(ps[:, col0 + f * T:col0 + (f + 1) * T], weight[:, t, f * P:(f + 1) * P],
                                         src[:, t, :], start=(t == 0), stop=(t == ET - 1))
                return last

            def turn(ps, src):
                for t in range(ET):
                    last = pe.transpose(ps[:, t * T:(t + 1) * T], src[:, t * P:(t + 1) * P], ident[:, :])
                return last

            def l0_use(section, c, name):
                b = c - 1
                if name == "xT":
                    pe.wait_ge(xhat_s, c + 1)
                    last = turn(scratch(section, b, name), xhat)
                elif name == "mixin":
                    pe.wait_ge(xin_s, c + 1)
                    ps = scratch(section, b, name)
                    for t in range(ET):
                        pe.matmul(ps[:, 0:T], w1_sb[:, t, 0:4 * XM], xin[:, t, :], start=(t == 0), stop=(t == ET - 1))
                    for t in range(ET):
                        last = pe.matmul(ps[0:XM, T:2 * T], w1_sb[:, t, 4 * XM:5 * XM], xin[:, t, :],
                                         start=(t == 0), stop=(t == ET - 1))
                elif name in ("mix0", "mix1", "mix2"):
                    if name == "mix0":
                        read(section, b, "mixin")
                    slots = MIX_USES[int(name[3])][1]
                    ps = scratch(section, b, name)
                    for k, slot in enumerate(slots):
                        m = MIX_ORDER[slot]
                        for t in range(ET):
                            w = w2a_sb[:, m, t * P:(t + 1) * P] if m < 4 else w2b_sb[:, t * P:(t + 1) * P]
                            v = xxx[:, :] if m < 4 else xxx4[:, :]
                            last = pe.matmul(ps[:, (k * ET + t) * T:(k * ET + t + 1) * T], w, v, start=True, stop=True)
                elif name == "dec1":
                    pe.wait_ge(x5_s, 3 * c + 1)
                    ps = scratch(section, b, name)
                    for t in range(ET):
                        last = pe.matmul(ps[0:XD, 0:T], dw1_sb[:, t, :], x5[:, SLOT_W, t, :], start=(t == 0), stop=(t == ET - 1))
                elif name == "dec2":
                    read(section, b, "dec1")
                    ps = scratch(section, b, name)
                    for t in range(ET):
                        last = pe.matmul(ps[:, t * T:(t + 1) * T], dw2_sb[:, t * P:(t + 1) * P], dtanh[:, :],
                                         start=True, stop=True)
                elif name == "kr":
                    pe.wait_ge(x5_s, 3 * c + 2)
                    ps = scratch(section, b, name)
                    channels_first(ps, l0_weight("Wk"), x5[:, SLOT_K])
                    last = channels_first(ps, l0_weight("Wr"), x5[:, SLOT_R], E)
                elif name == "vg":
                    pe.wait_ge(x5_s, 3 * c + 3)
                    ps = scratch(section, b, name)
                    tokens_first(ps, l0_weight("Wv"), x5[:, SLOT_V])
                    last = channels_first(ps, l0_weight("Wg"), x5[:, SLOT_G], E)
                elif name in ("vr0", "vr1", "vr2", "vr3"):
                    n = int(name[2])
                    pe.wait_ge(vrep_s, 4 * c + n + 1)
                    ps = scratch(section, b, name)
                    for d in range(4):
                        last = pe.transpose(ps[:, d * T:(d + 1) * T], vrep[:, n, d, :], ident[:, :])
                elif name == "red":
                    ps = scratch(section, b, name)
                    pe.wait_ge(bonus_s, c + 1)
                    for t in range(ET):
                        pe.matmul(ps[:, E + t * HT:E + (t + 1) * HT], bonus[:, t, :], head_ones[:, :], start=True, stop=True)
                    for n in range(4):
                        pe.wait_ge(rs_s, 4 * c + n + 1)
                        t, dh = n // 2, n % 2
                        for d in range(dh * 4, dh * 4 + 4):
                            dst = ps[:, t * P:(t + 1) * P].rearrange("p (h d) -> p h d", d=SD)[:, :, d]
                            last = pe.matmul(dst, kv[:, t, d, :], head_ones[:, :], start=True, stop=True)
                elif name == "attT":
                    pe.wait_ge(yhat_s, c + 1)
                    last = turn(scratch(section, b, name), yhat)
                elif name == "wo":
                    pe.wait_ge(ygT_s, c + 1)
                    last = tokens_first(scratch(section, b, name), l0_weight("Wo"), ygT)
                elif name == "x2T":
                    pe.wait_ge(xhat2_s, c + 1)
                    last = turn(scratch(section, b, name), xhat2)
                elif name == "kkrr":
                    pe.wait_ge(xkr_s, c + 1)
                    ps = scratch(section, b, name)
                    channels_first(ps, l0_weight("fWk"), xk)
                    last = tokens_first(ps, l0_weight("fWr"), xr, E)
                else:
                    assert name == "ffn"
                    pe.wait_ge(ksq_s, c + 1)
                    last = tokens_first(scratch(section, b, name), l0_weight("fWv"), ksq)
                last.then_inc(scr_ready, 1)

            def project(b, p):
                n = NP * b + p
                if p == 0:
                    pe.wait_ge(z_s, b + 1)
                    pe.wait_ge(u_s, b + 1)
                if not (isinstance(b, int) and n == 0):
                    pe.wait_ge(qk_s, 2 * n)
                for a in range(2):
                    for lt in range(ET):
                        dst = qk_ps[:, a, lt * P:(lt + 1) * P]
                        o = slice(a * HD + p * P, a * HD + (p + 1) * P)
                        pe.matmul(dst, wqkv_sb[:, lt, o], z_sb[:, lt * P:(lt + 1) * P], start=True, stop=False)
                        last = pe.matmul(dst, winj_sb[:, lt, o], u_sb[:, lt * P:(lt + 1) * P], start=False, stop=True)
                last.then_inc(proj_s, 1)

            def values(section, b, name):
                oh, lt = int(name[1]), int(name[2])
                ps = scratch(section, b, name)
                o = slice(2 * HD + oh * (HD // 2), 2 * HD + (oh + 1) * (HD // 2))
                pe.matmul(ps[:, :], z_sb[:, lt * P:(lt + 1) * P], wqkv_sb[:, lt, o], start=True, stop=False)
                pe.matmul(ps[:, :], u_sb[:, lt * P:(lt + 1) * P], winj_sb[:, lt, o], start=False, stop=True).then_inc(scr_ready, 1)

            def scores(section, b, p):
                pe.wait_ge(qk_s, 2 * (NP * b + p + 1))
                for h in range(2):
                    if p > 0 or section != "first":
                        pe.wait_ge(prob_s, 16 * b + (2 * p + h - 1))
                    rows = slice(h * DH, (h + 1) * DH)
                    for it in range(ET):
                        last = pe.matmul(s_ps[h][:, it, :], q_sb[rows, p % 2, it * P:(it + 1) * P], k_sb[rows, p % 2, :],
                                         start=True, stop=True)
                    last.then_inc(score_s, 1)

            def turn_probs(first, b, p):
                for h in range(2):
                    pe.wait_ge(prob_s, 16 * b + (2 * p + h + 1))
                    if not first:
                        pe.wait_ge(probT_s[h], NP * b + p)
                    for it in range(ET):
                        for jt in range(ET):
                            last = pe.transpose(t_ps[h][:, jt, it, :], prob[:, p % 2, h, it, jt * P:(jt + 1) * P], ident[:, :])
                    last.then_inc(turn_s, 1)

            def attend(first, b, p):
                if not first:
                    pe.wait_ge(attn_s, NP * b + p)
                for h in range(2):
                    pe.wait_ge(probT_s[h], NP * b + p + 1)
                    for it in range(ET):
                        for jt in range(ET):
                            last = pe.matmul(o_ps[:, h, it, 0:VW], probT[:, p % 2, h, jt, it, :], v1_sb[:, jt, 2 * p + h, :],
                                             start=(jt == 0), stop=(jt == ET - 1))
                last.then_inc(pv_s, 1)

            def turn_attn(section, b, name, entry):
                k = int(name[2])
                pe.wait_ge(attn_s, NP * entry + (2 * k + 2))
                ps = scratch(section, b, name)
                for a in range(2):
                    for it in range(ET):
                        last = pe.transpose(ps[:, (a * ET + it) * P:(a * ET + it + 1) * P],
                                            attn[:, it, (2 * k + a) * P:(2 * k + a + 1) * P], ident[:, :])
                last.then_inc(scr_ready, 1)

            def output(section, b):
                read(section, b, "AT3'")
                read(section, b, "AT2'")
                pe.wait_ge(zres_s, b)
                ps = scratch(section, b, "Y'")
                for lt in range(ET):
                    dst = ps[:, lt * P:(lt + 1) * P]
                    for p in range(NP):
                        pe.matmul(dst, attnT[:, p, lt * P:(lt + 1) * P], wo1_sb[:, p, :], start=(p == 0), stop=False)
                    pe.matmul(dst, zres[:, lt * P:(lt + 1) * P], ident[:, :], start=False, stop=False)
                    last = pe.matmul(dst, ones_row[:, :], bo_sb[:, :], start=False, stop=True)
                last.then_inc(scr_ready, 1)

            def output_turned(section, b):
                read(section, b, "Y'")
                ps = scratch(section, b, "OT'")
                for t in range(ET):
                    last = pe.transpose(ps[:, t * P:(t + 1) * P], yn[:, t, :], ident[:, :])
                last.then_inc(scr_ready, 1)

            L0_AT = {(0, "a"): ["xT"], (0, "b"): ["mixin"], (0, "c"): ["mix0"], (1, "a"): ["mix1"], (1, "b"): ["mix2"],
                     (2, "a"): ["dec1"], (2, "b"): ["dec2"], (2, "c"): ["kr"], (3, "a"): ["vg"], (3, "b"): ["vr0"],
                     (3, "c"): ["vr1"], (4, "a"): ["vr2"], (4, "b"): ["vr3"], (5, "c"): ["red"], (6, "a"): ["attT"],
                     (6, "b"): ["wo"], (6, "c"): ["x2T"], (7, "a"): ["kkrr"], (7, "b"): ["ffn"]}

            def step(section, b):
                def l0(slot, phase):
                    if section != "last":
                        for name in L0_AT.get((slot, phase), []):
                            l0_use(section, b + 1, name)

                old = section != "first"
                for p in range(NP):
                    scores(section, b, p)
                    l0(p, "a")
                    if old and p == 2:
                        turn_attn(section, b, "AT3'", b - 1)
                    if old and p == 3:
                        output(section, b)
                    if old and p == 4:
                        output_turned(section, b)
                    if p < NP - 1:
                        project(b, p + 1)
                    if p > 0:
                        turn_probs(section == "first" and p == 1, b, p - 1)
                    elif old:
                        turn_probs(False, b - 1, NP - 1)
                    if p == 6:
                        turn_attn(section, b, "AT1", b)
                    l0(p, "b")
                    if p > 1:
                        attend_values(section, b, p - 2)
                        attend(section == "first" and p == 2, b, p - 2)
                    elif old:
                        attend(False, b - 1, NP - 2 + p)
                    if p == 1:
                        values(section, b, "V00")
                        values(section, b, "V01")
                    if p == 3:
                        values(section, b, "V10")
                        values(section, b, "V11")
                    l0(p, "c")
                    if old and p == 0:
                        turn_attn(section, b, "AT2'", b - 1)
                    if p == 4:
                        turn_attn(section, b, "AT0", b)
                if section != "last":
                    project(b + 1, 0)

            def attend_values(section, b, p):
                if p in (0, 4):
                    read(section, b, f"V{p // 4}0")
                    read(section, b, f"V{p // 4}1")

            def tail():
                turn_probs(False, B - 1, NP - 1)
                attend(False, B - 1, NP - 2)
                turn_attn("tail", B, "AT2'", B - 1)
                attend(False, B - 1, NP - 1)
                turn_attn("tail", B, "AT3'", B - 1)
                output("tail", B)
                output_turned("tail", B)

            pe.wait_ge(setup, SETUP_STEPS)
            pe.wait_ge(in_l0a, 16 * 9)
            for name in L0_USES:
                if name == "wo":
                    pe.wait_ge(in_l0b, 16)
                l0_use("prologue", 0, name)
            pe.wait_ge(in_l1a, 32)
            project(0, 0)
            pe.wait_ge(in_l1b, 32)
            run_steps(pe, step, tail)
    return nc


def kernel(**inputs):
    import numpy as np
    import concourse.bacc as bacc
    from concourse.bass_utils import run_bass_kernel_spmd

    a = {k: np.asarray(v) for k, v in inputs.items()}
    l0 = {k[len("L0_xattn_"):]: v for k, v in a.items() if k.startswith("L0_xattn_")}
    l1 = {k[len("L1_xattn_"):]: v for k, v in a.items() if k.startswith("L1_xattn_")}

    def tiles(v):
        v = v.reshape(-1, ET, P)
        return np.moveaxis(v, 2, 0).reshape(P, -1)

    def rows(w):
        return np.moveaxis(w.reshape(ET, P, -1), 1, 0)

    parts = {
        "ln1_w": l0["ln1_w"], "ln1_b": l0["ln1_b"], "ln2_w": l0["ln2_w"], "ln2_b": l0["ln2_b"],
        "maa_x": l0["maa_x"], "maa": l0["maa_stack"], "decay": l0["time_decay"], "bonus": l0["faaaa"].reshape(E),
        "gn_w": l0["gn_w"], "gn_b": l0["gn_b"], "ffn_k": l0["ffn_maa_k"], "ffn_r": l0["ffn_maa_r"],
    }
    laid = {k: tiles(v) for k, v in parts.items()}
    laid["q_bias"] = l1["r_w_bias"].reshape(NP, P).T
    ctx_np = a["ctx_2048"]
    laid["prev"] = tiles(np.stack([ctx_np[:, 1, :], ctx_np[:, 0, :]]))
    arrays = {
        "x": a["x"],
        "ctx_in": ctx_np,
        "consts": np.concatenate([laid[name] for name, _ in CONSTS], axis=1),
        "state0": np.moveaxis(ctx_np[:, 2:2 + SD, :].reshape(B, ET, P, SD), 2, 0),
        "l0w": np.stack([rows(l0[n].T) for n in
                         ("Wk", "Wr", "Wv", "Wg", "Wo", "ffn_Wk", "ffn_Wr", "ffn_Wv")], axis=1),
        "maa_w1": rows(l0["maa_w1"]),
        "maa_w2": l0["maa_w2"].reshape(MIX * XM, E),
        "decay_w1": rows(l0["decay_w1"]),
        "decay_w2": l0["decay_w2"],
        "wqkv": np.stack([l1["Wqkv0"].T, l1["Wqkv1"].T], axis=1),
        "winj": np.stack([l1["Winj0"].T, l1["Winj1"].T], axis=1),
        "wo1": np.moveaxis(l1["Wo"].T.reshape(NP, P, P), 1, 0),
        "bo": l1["bo"].reshape(1, P),
    }
    arrays = {f"in_{k}": np.ascontiguousarray(v) for k, v in arrays.items()}
    nc = bacc.Bacc("TRN2", target_bir_lowering=False, num_devices=1)
    args = [nc.dram_tensor(k, v.shape, mybir.dt.from_np(v.dtype), kind="ExternalInput").ap() for k, v in arrays.items()]
    args.append(nc.dram_tensor("out_z", (B, T, E), F32, kind="ExternalOutput").ap())
    rwkv_then_attention(nc, *args)
    r = run_bass_kernel_spmd(nc, [arrays], core_ids=[0])
    return r.results[0]["out_z"]
```

```python
from contextlib import ExitStack

import concourse.bass as bass
from concourse import mybir

F32 = mybir.dt.float32
ALU = mybir.AluOpType
ACT = mybir.ActivationFunctionType
AX = mybir.AxisListType

P = 128
B = 8
T = 128
E = 256
ET = E // P
SD = 8
HT = P // SD
H0 = E // SD
MIX = 5
XM = 32
XD = 64
EPS = 1e-5
NH = 16
DH = 64
NP = NH // 2
HD = NH * DH
SCALE = DH ** -0.5
VW = DH + 1

MIX_ORDER = [1, 0, 2, 3, 4]
SLOT_W, SLOT_K, SLOT_V, SLOT_R, SLOT_G = range(MIX)
MIX_USES = [("mix0", [0, 1]), ("mix1", [2, 3]), ("mix2", [4])]

CONSTS = [("ln1_w", ET), ("ln1_b", ET), ("ln2_w", ET), ("ln2_b", ET), ("maa_x", ET), ("maa", MIX * ET),
          ("decay", ET), ("bonus", ET), ("gn_w", ET), ("gn_b", ET), ("ffn_k", ET), ("ffn_r", ET),
          ("q_bias", NP), ("bo", 1), ("prev", 2 * B * ET)]
COL, _n = {}, 0
for _name, _w in CONSTS:
    COL[_name] = _n
    _n += _w
NCONST = _n

L0W = ["Wk", "Wr", "Wv", "Wg", "Wo", "fWk", "fWr", "fWv"]

SCHEDULE = {
    (0, "start"): ["ln1"], (0, "a"): ["xT"], (0, "b"): ["mixin"], (0, "c"): ["mix0", "AT2'"],
    (1, "a"): ["mix1"], (1, "b"): ["mix2", "V00"], (1, "c"): ["V01", "dec1"],
    (2, "a"): ["AT3'", "dec2"], (2, "b"): ["kr"], (2, "c"): ["vg"],
    (3, "a"): ["vr0"], (3, "b"): ["vr1", "scan0"], (3, "c"): ["vr2", "scan1"],
    (4, "a"): ["vr3", "scan2"], (4, "b"): ["scan3", "Y'"], (4, "c"): ["red"],
    (5, "a"): ["V10", "AT0"], (5, "b"): ["V11", "hrstd"], (5, "c"): ["attT", "OT'"],
    (6, "a"): ["wo"], (6, "b"): ["AT1", "xhat2"], (6, "c"): ["x2T"],
    (7, "b"): ["kkrr"], (7, "c"): ["ffn"],
}
ORDER = [name for p in range(NP) for phase in ("start", "a", "b", "c")
         for name in SCHEDULE.get((p, phase), [])]
L1_STAGES = ["V00", "V01", "V10", "V11", "AT0", "AT1", "AT2'", "AT3'", "Y'", "OT'"]
NO_SCRATCH = ["ln1", "scan0", "scan1", "scan2", "scan3", "hrstd", "xhat2"]

STEP_USES = [name for name in ORDER if name not in NO_SCRATCH]
L0_USES = [name for name in STEP_USES if name not in L1_STAGES]
SECTIONS = {
    "prologue": list(L0_USES),
    "first": [u for u in STEP_USES if not u.endswith("'")],
    "loop": list(STEP_USES),
    "last": [u for u in STEP_USES if u not in L0_USES],
    "tail": ["AT2'", "AT3'", "Y'", "OT'"],
}
LOOP_STEPS = B - 2
SETUP_STEPS = 12 + SD


def scratch_plan():
    plan, total, of_bank = {}, 0, [0, 0]
    for section, uses in SECTIONS.items():
        times = LOOP_STEPS if section == "loop" else 1
        steps = (len(uses), [len(uses[n::2]) for n in range(2)])
        for n, name in enumerate(uses):
            bank = n % 2
            plan[section, name] = (bank, total + n, of_bank[bank] + n // 2,
                                   steps[0] if section == "loop" else 0,
                                   steps[1][bank] if section == "loop" else 0)
        total += times * steps[0]
        of_bank = [of_bank[n] + times * steps[1][n] for n in range(2)]
    return plan


def rwkv_then_attention(nc, x, ctx_in, consts, state0, l0w, maa_w1, maa_w2, decay_w1, decay_w2,
                        wqkv, winj, wo1, out):
    plan = scratch_plan()
    with ExitStack() as stack:
        def sb(name, shape, dt=F32):
            return stack.enter_context(nc.sbuf_tensor(name, shape, dt))

        def psum(name, shape, dt=F32):
            return stack.enter_context(nc.psum_tensor(name, shape, dt))

        def sem(name):
            return stack.enter_context(nc.semaphore(name))

        cst = sb("cst", [P, NCONST])
        s0_all = sb("s0_all", [P, B, ET, SD])
        l0w_sb = sb("l0w_sb", [P, len(L0W), ET, E])
        w1_sb = sb("w1_sb", [P, ET, MIX * XM])
        w2a_sb = sb("w2a_sb", [P, 4, E])
        w2b_sb = sb("w2b_sb", [XM, E])
        dw1_sb = sb("dw1_sb", [P, ET, XD])
        dw2_sb = sb("dw2_sb", [XD, E])
        wqkv_sb = sb("wqkv_sb", [P, 2, 3 * HD])
        winj_sb = sb("winj_sb", [P, 2, 3 * HD])
        wo1_sb = sb("wo1_sb", [P, NP, P])
        ident = sb("ident", [P, P])
        head_ones = sb("head_ones", [P, HT])
        select = sb("select", [P, SD, HT, SD])
        minus_half = sb("minus_half", [P, H0])
        one = sb("one", [P, 1])
        eps_row = sb("eps_row", [P, ET])
        carrier = sb("carrier", [P, 2])
        q_bias = sb("q_bias", [P, NP])

        x_sb = sb("x_sb", [P, E])
        st1 = sb("st1", [P, 6])
        mv1 = sb("mv1", [P, 2])
        ve1 = sb("ve1", [P, 1])
        rstd1 = sb("rstd1", [P, 1])
        xhat = sb("xhat", [P, E])
        xn = sb("xn", [P, ET, T + 1])
        sx = sb("sx", [P, ET, T])
        xin = sb("xin", [P, ET, T])
        xxx = sb("xxx", [P, T])
        xxx4 = sb("xxx4", [XM, T])
        x5 = sb("x5", [P, MIX, ET, T])
        dtanh = sb("dtanh", [XD, T])
        dexp = sb("dexp", [P, ET, T])
        w_sb = sb("w_sb", [P, ET, T])
        kr_sb = sb("kr_sb", [P, 2, ET, T])
        bonus = sb("bonus", [P, ET, T])
        v_sb = sb("v_sb", [P, E])
        vrep = sb("vrep", [P, 4, 4, P])
        g_sb = sb("g_sb", [P, ET, T])
        g_tanh = sb("g_tanh", [P, ET, T])
        gate = sb("gate", [P, ET, T])
        kv = sb("kv", [P, ET, SD, T])
        states = sb("states", [P, ET, SD, T + 1])
        bonus_v = sb("bonus_v", [P, E])
        att = sb("att", [P, E])
        hsum = sb("hsum", [P, H0])
        cent = sb("cent", [P, E])
        sq = sb("sq", [P, E])
        hsq = sb("hsq", [P, H0])
        hve = sb("hve", [P, H0])
        hrstd = sb("hrstd", [P, H0])
        yhat = sb("yhat", [P, E])
        yT = sb("yT", [P, ET, T])
        ygT = sb("ygT", [P, ET, T])
        x1 = sb("x1", [P, E])
        st2 = sb("st2", [P, 6])
        mv2 = sb("mv2", [P, 2])
        ve2 = sb("ve2", [P, 1])
        rstd2 = sb("rstd2", [P, 1])
        xhat2 = sb("xhat2", [P, E])
        xn2 = sb("xn2", [P, ET, T + 1])
        sx2 = sb("sx2", [P, ET, T])
        xk = sb("xk", [P, ET, T])
        xr = sb("xr", [P, ET, T])
        krelu = sb("krelu", [P, ET, T])
        ksq = sb("ksq", [P, ET, T])
        rtanh = sb("rtanh", [P, E])
        rsig = sb("rsig", [P, E])
        ffn_r = sb("ffn_r", [P, E])

        z_sb = sb("z_sb", [P, E])
        zres = sb("zres", [P, E])
        u_in = sb("u_in", [P, E])
        u_sb = sb("u_sb", [P, E])
        q_sb = sb("q_sb", [P, 2, E])
        k_sb = sb("k_sb", [P, 2, E])
        v1_sb = sb("v1_sb", [P, ET, NH, VW])
        nmax = sb("nmax", [P, 2, 2, ET])
        prob = sb("prob", [P, 2, 2, ET, E])
        probT = sb("probT", [P, 2, 2, ET, ET, P])
        rden = sb("rden", [P, 2, ET, 1])
        attn = sb("attn", [P, ET, HD])
        attnT = sb("attnT", [P, NP, E])
        st3 = sb("st3", [P, ET, 6])
        mv3 = sb("mv3", [P, ET, 2])
        ve3 = sb("ve3", [P, ET])
        rstd3 = sb("rstd3", [P, ET])
        yn = sb("yn", [P, ET, P])
        o_sb = sb("o_sb", [P, E])

        qk_ps = psum("qk_ps", [P, 2, E])
        s_ps = [psum(f"s_ps{h}", [P, ET, E]) for h in range(2)]
        t_ps = [psum(f"t_ps{h}", [P, ET, ET, P]) for h in range(2)]
        o_ps = psum("o_ps", [P, 2, ET, P])
        scr = [psum(f"scr{n}", [P, 512]) for n in range(2)]

        x_in, u_loaded, out_stored = sem("x_in"), sem("u_loaded"), sem("out_stored")
        in_cst, in_l0a, in_l0b, in_l1a, in_l1b = (sem(f"in_{n}") for n in ("cst", "l0a", "l0b", "l1a", "l1b"))
        setup = sem("setup")
        bias_scaled = sem("bias_scaled")
        scr_ready = sem("scr_ready")
        scr_free = [sem(f"scr_free{n}") for n in range(2)]
        stats1, mean1, eps1, rstd1_s, xhat_s = (sem(n) for n in ("stats1", "mean1", "eps1", "rstd1_s", "xhat_s"))
        prev1_s, sx_s, xin_s = (sem(n) for n in ("prev1_s", "sx_s", "xin_s"))
        x5_s = sem("x5_s")
        w_s, bonus_s, gate_s = sem("w_s"), sem("bonus_s"), sem("gate_s")
        s0_s = sem("s0_s")
        vrep_s = sem("vrep_s")
        scan_s = sem("scan_s")
        rs_s = sem("rs_s")
        gn_s = sem("gn_s")
        hrstd_s, yhat_s, ygT_s = (sem(n) for n in ("hrstd_s", "yhat_s", "ygT_s"))
        stats2, mean2, eps2, rstd2_s, xhat2_s = (sem(n) for n in ("stats2", "mean2", "eps2", "rstd2_s", "xhat2_s"))
        prev2_s, sx2_s, xkr_s = (sem(n) for n in ("prev2_s", "sx2_s", "xkr_s"))
        ksq_s, rsig_s, ffnr_s, z_s, zres_s, u_s = (sem(n) for n in ("ksq_s", "rsig_s", "ffnr_s", "z_s", "zres_s", "u_s"))
        proj_s = sem("proj_s")
        qk_s = sem("qk_s")
        score_s = sem("score_s")
        max_s = sem("max_s")
        prob_s = sem("prob_s")
        turn_s = sem("turn_s")
        probT_s = [sem("probT_s0"), sem("probT_s1")]
        pv_s = sem("pv_s")
        rden_s = sem("rden_s")
        attn_s = sem("attn_s")
        stats3, mean3, eps3, rstd3_s, yn_s = (sem(n) for n in ("stats3", "mean3", "eps3", "rstd3_s", "yn_s"))

        block = stack.enter_context(nc.Block())

        def col(name, n=0):
            return cst[:, COL[name] + n:COL[name] + n + 1]

        def l0_weight(name):
            return l0w_sb[:, L0W.index(name), :, :]

        def use(section, name, b):
            bank, before, bank_before, step, bank_step = plan[section, name]
            if section != "loop":
                return bank, before + 1, bank_before
            return bank, b * step + (before + 1 - step), b * bank_step + (bank_before - bank_step)

        def included(section, name):
            if name in L1_STAGES:
                return section in ("loop", "last") or (section == "first" and not name.endswith("'")) or (
                    section == "tail" and name.endswith("'"))
            return section in ("prologue", "first", "loop")

        def stages(section, slot, phase):
            return [name for name in SCHEDULE.get((slot, phase), []) if included(section, name)]

        def run_steps(eng, step, tail=None):
            step("first", 0)
            with eng.Fori(1, B - 1) as b:
                step("loop", b)
            step("last", B - 1)
            if tail:
                tail()

        @block.sync
        def _(sp):
            sp.dma_start(x_sb[:, :], x[0]).then_inc(x_in, 16)
            sp.dma_start(cst[:, :], consts).then_inc(in_cst, 16)
            sp.dma_start(w1_sb[:, :, :], maa_w1).then_inc(in_l0a, 16)
            sp.wait_ge(setup, 1)
            for m in range(4):
                rows = slice(m * XM, (m + 1) * XM)
                sp.dma_start(w2a_sb[rows, m, :], maa_w2[rows, :]).then_inc(in_l0a, 16)
            sp.dma_start(w2b_sb[:, :], maa_w2[4 * XM:5 * XM, :]).then_inc(in_l0a, 16)
            sp.dma_start(dw1_sb[:, :, :], decay_w1).then_inc(in_l0a, 16)
            sp.dma_start(dw2_sb[:, :], decay_w2).then_inc(in_l0a, 16)
            sp.dma_start(s0_all[:, :, :, :], state0).then_inc(in_cst, 16)
            sp.dma_start(l0w_sb[:, 0:4, :, :], l0w[:, 0:4]).then_inc(in_l0a, 16)
            sp.dma_start(l0w_sb[:, 4:8, :, :], l0w[:, 4:8]).then_inc(in_l0b, 16)
            sp.dma_start(u_in[:, :], ctx_in[0]).then_inc(u_loaded, 16)
            sp.dma_start(wqkv_sb[:, :, :], wqkv).then_inc(in_l1a, 16)
            sp.dma_start(winj_sb[:, :, :], winj).then_inc(in_l1a, 16)
            sp.dma_start(wo1_sb[:, :, :], wo1).then_inc(in_l1b, 16)

            def load_next(section, b):
                bank, _, before = use(section, "wo", b - 1)
                sp.wait_ge(scr_free[bank], before + 1)
                sp.dma_start(x_sb[:, :], x[b + 1]).then_inc(x_in, 16)
                sp.wait_ge(u_s, b + 1)
                sp.dma_start(u_in[:, :], ctx_in[b + 1]).then_inc(u_loaded, 16)

            def store(section, b):
                bank, _, before = use(section, "OT'", b + 1)
                sp.wait_ge(scr_free[bank], before + 1)
                sp.dma_start(out[b], o_sb[:, :]).then_inc(out_stored, 16)

            load_next("prologue", 0)
            load_next("first", 1)
            with sp.Fori(1, B - 2) as b:
                store("loop", b - 1)
                load_next("loop", b + 1)
            store("loop", B - 3)
            store("last", B - 2)
            store("tail", B - 1)
            sp.wait_ge(out_stored, 16 * B)

        @block.gpsimd
        def _(pool):
            done = 0

            def chained(ins):
                nonlocal done
                done += 1
                ins.then_inc(setup, 1)
                pool.wait_ge(setup, done)

            chained(pool.memset(w2a_sb[:, :, :], 0.0))
            chained(pool.memset(ident[:, :], 0.0))
            chained(pool.affine_select(out=ident[:, :], in_=ident[:, :], compare_op=ALU.not_equal, fill=1.0,
                                       base=0, pattern=[[-1, P]], channel_multiplier=1))
            chained(pool.memset(head_ones[:, :], 1.0))
            chained(pool.affine_select(out=head_ones[:, :], in_=head_ones[:, :], compare_op=ALU.is_ge, fill=0.0,
                                       base=0, pattern=[[-SD, HT]], channel_multiplier=1))
            chained(pool.affine_select(out=head_ones[:, :], in_=head_ones[:, :], compare_op=ALU.is_ge, fill=0.0,
                                       base=SD - 1, pattern=[[SD, HT]], channel_multiplier=-1))
            chained(pool.memset(minus_half[:, :], -0.5))
            chained(pool.memset(select[:, :, :, :], 0.0))
            for d in range(SD):
                chained(pool.tensor_copy(select[:, d, :, d], head_ones[:, :]))
            chained(pool.memset(one[:, :], 1.0))
            chained(pool.memset(eps_row[:, :], EPS))
            chained(pool.memset(carrier[:, :], 0.0))
            chained(pool.memset(v1_sb[:, :, :, DH:VW], 1.0))
            pool.wait_ge(in_cst, 32)
            pool.tensor_scalar(q_bias[:, :], cst[:, COL["q_bias"]:COL["q_bias"] + NP], SCALE, None,
                               ALU.mult).then_inc(bias_scaled, 1)

            def copy(dst, src, shape):
                ones = one[:, :]
                while len(ones.shape) < len(shape):
                    ones = ones[:, None]
                return pool.tensor_tensor(dst, src, ones.to_broadcast(shape), ALU.mult)

            def rsqrt(var, ve, rstd, n, wait_var, eps_sem, rstd_sem, val):
                pool.wait_ge(wait_var, val)
                pool.tensor_tensor(ve, var, eps_row[:, 0:n], ALU.add).then_inc(eps_sem, 1)
                pool.wait_ge(eps_sem, val)
                pool.tensor_tensor(rstd, ve, minus_half[:, 0:n], ALU.pow).then_inc(rstd_sem, 1)

            def shifted_rows(c):
                n = COL["prev"]
                prev = cst[:, n:n + 2 * B * ET].rearrange("p (r b t) -> p r b t", r=2, b=B)
                pool.tensor_copy(xn[:, :, 0:1], prev[:, 0, bass.ds(c, 1), :].rearrange("p b t -> p t b")).then_inc(prev1_s, 1)
                pool.tensor_copy(xn2[:, :, 0:1], prev[:, 1, bass.ds(c, 1), :].rearrange("p b t -> p t b")).then_inc(prev2_s, 1)

            def first_states(c):
                pool.tensor_copy(states[:, :, :, 0:1],
                                 s0_all[:, bass.ds(c, 1), :, :].rearrange("p b t d -> p t d b")).then_inc(s0_s, 1)

            def mix_add(section, c, n):
                name, slots = MIX_USES[n]
                bank, _, before = use(section, name, c - 1)
                pool.wait_ge(scr_free[bank], before + 1)
                a, z = slots[0], slots[-1] + 1
                xb = xn[:, None, :, 1:T + 1].to_broadcast([P, z - a, ET, T])
                pool.tensor_tensor(x5[:, a:z, :, :], x5[:, a:z, :, :], xb, ALU.add).then_inc(x5_s, 1)

            def spread_v(section, c):
                bank, _, before = use(section, "vg", c - 1)
                pool.wait_ge(scr_free[bank], before + 1)
                for n in range(4):
                    t, dh = n // 2, n % 2
                    src = v_sb[:, t * P:(t + 1) * P].rearrange("p (h d) -> p d h", d=SD)[:, dh * 4:dh * 4 + 4, :]
                    dst = vrep[:, n, :, :].rearrange("p d (h k) -> p d h k", k=SD)
                    src = src[:, :, :, None].to_broadcast([P, 4, HT, SD])
                    if n == 0:
                        last = copy(dst, src, [P, 4, HT, SD])
                    else:
                        last = pool.tensor_copy(dst, src)
                    last.then_inc(vrep_s, 1)

            def receive(c, n):
                t, dh = n // 2, n % 2
                d = slice(dh * 4, dh * 4 + 4)
                pool.wait_ge(scan_s, 4 * c + n + 1)
                r = kr_sb[:, 1, t:t + 1, :].to_broadcast([P, 4, T])
                pool.tensor_tensor(kv[:, t, d, :], states[:, t, d, 0:T], r, ALU.mult).then_inc(rs_s, 1)

            def stage(section, b, name):
                c = b + 1
                if name == "ln1":
                    rsqrt(mv1[:, 1:2], ve1[:, :], rstd1[:, :], 1, mean1, eps1, rstd1_s, c + 1)
                    shifted_rows(c)
                if name in ("mix0", "mix1", "mix2"):
                    mix_add(section, c, int(name[3]))
                if name == "vg":
                    first_states(c)
                    spread_v(section, c)
                if name in ("scan0", "scan1", "scan2", "scan3"):
                    receive(c, int(name[4]))
                if name == "red":
                    pool.wait_ge(gn_s, 7 * c + 7)
                    pool.tensor_tensor(hrstd[:, :], hve[:, :], minus_half[:, :], ALU.pow).then_inc(hrstd_s, 1)
                if name == "wo":
                    rsqrt(mv2[:, 1:2], ve2[:, :], rstd2[:, :], 1, mean2, eps2, rstd2_s, c + 1)
                if name == "Y'":
                    rsqrt(mv3[:, :, 1], ve3[:, :], rstd3[:, :], ET, mean3, eps3, rstd3_s, b)

            def keep_z(section, b):
                if section != "first":
                    pool.wait_ge(scr_ready, use(section, "Y'", b)[1])
                pool.wait_ge(z_s, b + 1)
                pool.tensor_tensor(zres[:, :], z_sb[:, :], col("bo").to_broadcast([P, E]), ALU.add).then_inc(zres_s, 1)

            def take_u(b):
                pool.wait_ge(proj_s, NP * b)
                pool.wait_ge(u_loaded, 16 * (b + 1))
                copy(u_sb[:, :], u_in[:, :], [P, E]).then_inc(u_s, 1)

            def step(section, b):
                for name in ORDER:
                    if included(section, name):
                        stage(section, b, name)
                    if name == "OT'":
                        keep_z(section, b)
                    if name == "x2T" and section != "last":
                        take_u(b + 1)

            pool.wait_ge(u_loaded, 16)
            pool.tensor_copy(u_sb[:, :], u_in[:, :]).then_inc(u_s, 1)
            for name in ORDER:
                if included("prologue", name):
                    stage("prologue", -1, name)
            run_steps(pool, step, lambda: stage("tail", B, "Y'"))

        @block.scalar
        def _(act):
            def l0_scratch(section, c, name):
                bank, ready, _ = use(section, name, c - 1)
                act.wait_ge(scr_ready, ready)
                return scr[bank], scr_free[bank]

            def mix_tanh(section, c):
                ps, free = l0_scratch(section, c, "mixin")
                act.activation(xxx[:, :], ps[:, 0:T], ACT.Tanh)
                act.activation(xxx4[:, :], ps[0:XM, T:2 * T], ACT.Tanh).then_inc(free, 1)

            def decay_tanh(section, c):
                ps, free = l0_scratch(section, c, "dec1")
                act.activation(dtanh[:, :], ps[0:XD, 0:T], ACT.Tanh).then_inc(free, 1)

            def decay_exp(section, c):
                ps, free = l0_scratch(section, c, "dec2")
                for t in range(ET):
                    last = act.activation(dexp[:, t, :], ps[:, t * T:(t + 1) * T], ACT.Exp, bias=col("decay", t))
                last.then_inc(free, 1)
                _, _, before = use(section, "dec2", c - 1)
                act.wait_ge(free, before + 1)
                act.activation(w_sb[:, :, :], dexp[:, :, :], ACT.Exp, scale=-1.0).then_inc(w_s, 1)

            def key_receptance(section, c):
                ps, free = l0_scratch(section, c, "kr")
                act.activation(kr_sb[:, :, :, :], ps[:, :].rearrange("p (a t n) -> p a t n", a=2, t=ET),
                               ACT.Copy).then_inc(free, 1)

            def value_gate(section, c):
                ps, free = l0_scratch(section, c, "vg")
                g = ps[:, E:2 * E].rearrange("p (t n) -> p t n", t=ET)
                act.activation(v_sb[:, :], ps[:, 0:E], ACT.Copy)
                act.activation(g_sb[:, :, :], g, ACT.Copy)
                act.activation(g_tanh[:, :, :], g, ACT.Tanh, scale=0.5).then_inc(free, 1)

            def norm_affine(section, c):
                ps, free = l0_scratch(section, c, "attT")
                for t in range(ET):
                    last = act.activation(yT[:, t, :], ps[:, t * T:(t + 1) * T], ACT.Identity,
                                          scale=col("gn_w", t), bias=col("gn_b", t))
                last.then_inc(free, 1)

            def ffn_act(section, c):
                ps, free = l0_scratch(section, c, "kkrr")
                act.activation(krelu[:, :, :], ps[:, 0:E].rearrange("p (t n) -> p t n", t=ET),
                               ACT.Relu)
                act.activation(rtanh[:, :], ps[:, E:2 * E], ACT.Tanh, scale=0.5).then_inc(free, 1)

            def exps(g, p, h):
                par = p % 2
                act.wait_ge(max_s, 16 * g + 2 * p + h + 1)
                for it in range(ET):
                    last = act.activation(prob[:, par, h, it, :], s_ps[h][:, it, :], ACT.Exp,
                                          bias=nmax[:, par, h, it:it + 1])
                last.then_inc(prob_s, 1)

            def turned(b, p):
                act.wait_ge(turn_s, 16 * b + 2 * p + 2)
                act.activation(probT[:, p % 2, 1, :, :, :], t_ps[1][:, :, :, :], ACT.Copy).then_inc(probT_s[1], 1)

            def values(section, b, name):
                bank, ready, _ = use(section, name, b)
                act.wait_ge(scr_ready, ready)
                oh, lt = int(name[1]), int(name[2])
                act.activation(v1_sb[:, lt, 8 * oh:8 * oh + 8, 0:DH],
                               scr[bank][:, :].rearrange("p (h d) -> p h d", h=8), ACT.Copy).then_inc(scr_free[bank], 1)

            def stage(section, b, name):
                parts = {"mixin": mix_tanh, "dec1": decay_tanh, "dec2": decay_exp, "kr": key_receptance,
                         "vg": value_gate, "attT": norm_affine, "kkrr": ffn_act}
                if name in parts:
                    parts[name](section, b + 1)
                if name.startswith("V"):
                    values(section, b, name)

            def step(section, b):
                for p in range(NP):
                    if p == 0 and section != "first":
                        turned(b - 1, NP - 1)
                    exps(b, p, 0)
                    exps(b, p, 1)
                    for name in stages(section, p, "a"):
                        stage(section, b, name)
                    if p > 0:
                        turned(b, p - 1)
                    for name in stages(section, p, "b") + stages(section, p, "c"):
                        stage(section, b, name)

            act.wait_ge(in_cst, 32)
            for name in ORDER:
                if included("prologue", name):
                    stage("prologue", -1, name)
            run_steps(act, step, lambda: turned(B - 1, NP - 1))

        @block.vector
        def _(dve):
            def wait_apart(s, val):
                dve.wait_ge(s, val)
                dve.tensor_copy(carrier[:, 1:2], carrier[:, 0:1])

            def scratch(section, b, name):
                bank, ready, _ = use(section, name, b)
                dve.wait_ge(scr_ready, ready)
                return scr[bank], scr_free[bank]

            def layer_stats(src, wait, val, st, mv, st_sem, mv_sem, n):
                dve.wait_ge(wait, val)
                dve.bn_stats(st, src).then_inc(st_sem, 1)
                wait_apart(st_sem, n)
                dve.bn_aggr(mv, st).then_inc(mv_sem, 1)

            def normalise(dst, src, mv, rstd, wait, n, ready):
                dve.wait_ge(wait, n)
                dve.tensor_scalar(dst, src, mv[:, 0:1], rstd[:, 0:1], ALU.subtract, ALU.mult).then_inc(ready, 1)

            def shift_in(section, c, name, dst, ln, prev, diff, diff_sem):
                ps, free = scratch(section, c - 1, name)
                for t in range(ET):
                    last = dve.tensor_scalar(dst[:, t, 1:T + 1], ps[:, t * T:(t + 1) * T],
                                             col(ln + "_w", t), col(ln + "_b", t), ALU.mult, ALU.add)
                last.then_inc(free, 1)
                dve.wait_ge(prev, c + 1)
                dve.wait_ge(free, use(section, name, c - 1)[2] + 1)
                dve.tensor_tensor(diff[:, :, :], dst[:, :, 0:T], dst[:, :, 1:T + 1], ALU.subtract).then_inc(diff_sem, 1)
                dve.wait_ge(diff_sem, c + 1)

            def mix_in(c):
                for t in range(ET):
                    last = dve.scalar_tensor_tensor(xin[:, t, :], sx[:, t, :], col("maa_x", t), xn[:, t, 1:T + 1],
                                                    ALU.mult, ALU.add)
                last.then_inc(xin_s, 1)

            def mixes(section, c, n):
                name, slots = MIX_USES[n]
                ps, free = scratch(section, c - 1, name)
                for k, slot in enumerate(slots):
                    for t in range(ET):
                        last = dve.scalar_tensor_tensor(
                            x5[:, slot, t, :], ps[:, (k * ET + t) * T:(k * ET + t + 1) * T],
                            col("maa", MIX_ORDER[slot] * ET + t), sx[:, t, :], ALU.add, ALU.mult)
                last.then_inc(free, 1)

            def bonus_rk(section, c):
                bank, _, before = use(section, "kr", c - 1)
                dve.wait_ge(scr_free[bank], before + 1)
                for t in range(ET):
                    last = dve.scalar_tensor_tensor(bonus[:, t, :], kr_sb[:, 1, t, :], col("bonus", t),
                                                    kr_sb[:, 0, t, :], ALU.mult, ALU.mult)
                last.then_inc(bonus_s, 1)

            def make_gate(section, c):
                bank, _, before = use(section, "vg", c - 1)
                dve.wait_ge(scr_free[bank], before + 1)
                dve.scalar_tensor_tensor(gate[:, :, :], g_tanh[:, :, :], 1.0, g_sb[:, :, :],
                                         ALU.add, ALU.mult).then_inc(gate_s, 1)

            def key_value(section, c, n):
                t, dh = n // 2, n % 2
                ps, free = scratch(section, c - 1, f"vr{n}")
                k = kr_sb[:, 0, t:t + 1, :].to_broadcast([P, 4, T])
                dve.tensor_tensor(kv[:, t, dh * 4:dh * 4 + 4, :], ps[:, :].rearrange("p (d n) -> p d n", d=4), k,
                                  ALU.mult).then_inc(free, 1)

            def scans(section, c, n):
                t, dh = n // 2, n % 2
                bank, _, before = use(section, f"vr{n}", c - 1)
                dve.wait_ge(scr_free[bank], before + 1)
                if n == 0:
                    dve.wait_ge(w_s, c + 1)
                    dve.wait_ge(s0_s, c + 1)
                for d in range(dh * 4, dh * 4 + 4):
                    last = dve.tensor_tensor_scan(states[:, t, d, 1:T + 1], w_sb[:, t, :], kv[:, t, d, :],
                                                  states[:, t, d, 0:1], ALU.mult, ALU.add)
                last.then_inc(scan_s, 1)

            def group_norm(section, c):
                ps, free = scratch(section, c - 1, "red")
                n = 7 * c

                dve.tensor_tensor(heads(bonus_v[:, :]), heads(v_sb[:, :]), spread(ps[:, E:E + H0]), ALU.mult).then_inc(gn_s, 1)
                dve.wait_ge(gn_s, n + 1)
                dve.tensor_tensor(att[:, :], ps[:, 0:E], bonus_v[:, :], ALU.add).then_inc(free, 1)
                dve.wait_ge(free, use(section, "red", c - 1)[2] + 1)
                dve.tensor_reduce(hsum[:, :], heads(att[:, :]), AX.X, ALU.add).then_inc(gn_s, 1)
                dve.wait_ge(gn_s, n + 2)
                dve.scalar_tensor_tensor(heads(cent[:, :]), spread(hsum[:, :]), -1.0 / SD, heads(att[:, :]),
                                         ALU.mult, ALU.add).then_inc(gn_s, 1)
                dve.wait_ge(gn_s, n + 3)
                dve.tensor_tensor(sq[:, :], cent[:, :], cent[:, :], ALU.mult).then_inc(gn_s, 1)
                dve.wait_ge(gn_s, n + 4)
                dve.tensor_reduce(hsq[:, :], heads(sq[:, :]), AX.X, ALU.add).then_inc(gn_s, 1)
                dve.wait_ge(gn_s, n + 5)
                dve.tensor_scalar(hve[:, :], hsq[:, :], 1.0 / SD, EPS, ALU.mult, ALU.add).then_inc(gn_s, 2)

            def heads(a):
                return a.rearrange("p (h d) -> p h d", d=SD)

            def spread(a):
                return a.rearrange("p (h o) -> p h o", o=1).to_broadcast([P, H0, SD])

            def group_normed(c):
                dve.wait_ge(hrstd_s, c + 1)
                dve.tensor_tensor(heads(yhat[:, :]), heads(cent[:, :]), spread(hrstd[:, :]), ALU.mult).then_inc(yhat_s, 1)

            def gated(section, c):
                bank, _, before = use(section, "attT", c - 1)
                dve.wait_ge(scr_free[bank], before + 1)
                dve.scalar_tensor_tensor(ygT[:, :, :], gate[:, :, :], 0.5, yT[:, :, :], ALU.mult,
                                         ALU.mult).then_inc(ygT_s, 1)

            def residual1(section, c):
                ps, free = scratch(section, c - 1, "wo")
                dve.tensor_tensor(x1[:, :], ps[:, 0:E], x_sb[:, :], ALU.add).then_inc(free, 1)
                layer_stats(x1[:, :], free, use(section, "wo", c - 1)[2] + 1, st2[:, :], mv2[:, :], stats2, mean2, c + 1)

            def residual1_normed(c):
                normalise(xhat2[:, :], x1[:, :], mv2, rstd2, rstd2_s, c + 1, xhat2_s)

            def ffn_in(section, c):
                shift_in(section, c, "x2T", xn2, "ln2", prev2_s, sx2, sx2_s)
                for dst, name in ((xk, "ffn_k"), (xr, "ffn_r")):
                    for t in range(ET):
                        last = dve.scalar_tensor_tensor(dst[:, t, :], sx2[:, t, :], col(name, t),
                                                        xn2[:, t, 1:T + 1], ALU.mult, ALU.add)
                last.then_inc(xkr_s, 1)

            def ffn_mid(section, c):
                bank, _, before = use(section, "kkrr", c - 1)
                dve.wait_ge(scr_free[bank], before + 1)
                dve.tensor_tensor(ksq[:, :, :], krelu[:, :, :], krelu[:, :, :], ALU.mult).then_inc(ksq_s, 1)
                dve.tensor_scalar(rsig[:, :], rtanh[:, :], 0.5, 0.5, ALU.mult, ALU.add).then_inc(rsig_s, 1)

            def make_z(section, c):
                ps, free = scratch(section, c - 1, "ffn")
                dve.wait_ge(rsig_s, c + 1)
                dve.tensor_tensor(ffn_r[:, :], ps[:, 0:E], rsig[:, :], ALU.mult).then_inc(free, 1)
                dve.wait_ge(free, use(section, "ffn", c - 1)[2] + 1)
                if section != "prologue":
                    dve.wait_ge(proj_s, NP * c)
                    dve.wait_ge(zres_s, c)
                dve.tensor_tensor(z_sb[:, :], ffn_r[:, :], x1[:, :], ALU.add).then_inc(z_s, 1)

            def qk_out(g, p):
                par = p % 2
                dve.wait_ge(proj_s, NP * g + p + 1)
                dve.tensor_scalar(q_sb[:, par, :], qk_ps[:, 0, :], SCALE, q_bias[:, p:p + 1], ALU.mult,
                                  ALU.add).then_inc(qk_s, 1)
                dve.tensor_copy(k_sb[:, par, :], qk_ps[:, 1, :]).then_inc(qk_s, 1)

            def maxes(b, p, h):
                dve.wait_ge(score_s, 16 * b + 2 * p + h + 1)
                dve.tensor_reduce(nmax[:, p % 2, h, :], s_ps[h][:, :, :], AX.X, ALU.max, negate=True).then_inc(max_s, 1)

            def turned(b, p):
                dve.wait_ge(turn_s, 16 * b + 2 * p + 1)
                dve.tensor_copy(probT[:, p % 2, 0, :, :, :], t_ps[0][:, :, :, :]).then_inc(probT_s[0], 1)

            def attended(b, p):
                dve.wait_ge(pv_s, NP * b + p + 1)
                dve.reciprocal(rden[:, :, :, :], o_ps[:, :, :, DH:VW]).then_inc(rden_s, 1)
                dve.wait_ge(rden_s, NP * b + p + 1)
                dst = attn[:, :, 2 * p * DH:2 * (p + 1) * DH].rearrange("p i (h d) -> p h i d", h=2)
                dve.tensor_tensor(dst, o_ps[:, :, :, 0:DH], rden[:, :, :, :].to_broadcast([P, 2, ET, DH]),
                                  ALU.mult).then_inc(attn_s, 1)

            def attention_turned(section, b, name):
                ps, free = scratch(section, b, name)
                k = int(name[2])
                dve.tensor_copy(attnT[:, 2 * k:2 * k + 2, :], ps[:, :].rearrange("p (a n) -> p a n", a=2)).then_inc(free, 1)

            def finish(section, b):
                ps, free = scratch(section, b, "Y'")
                y = ps[:, 0:E].rearrange("p (t n) -> p t n", t=ET)
                for t in range(ET):
                    last = dve.bn_stats(st3[:, t, :], y[:, t, :])
                    last.then_inc(stats3, 1)
                wait_apart(stats3, 2 * b)
                for t in range(ET):
                    last = dve.bn_aggr(mv3[:, t, :], st3[:, t, :])
                last.then_inc(mean3, 1)

            def finish_normed(section, b):
                bank, _, before = use(section, "Y'", b)
                y = scr[bank][:, 0:E].rearrange("p (t n) -> p t n", t=ET)
                dve.wait_ge(rstd3_s, b)
                for t in range(ET):
                    last = dve.tensor_scalar(yn[:, t, :], y[:, t, :], mv3[:, t, 0:1], rstd3[:, t:t + 1],
                                             ALU.subtract, ALU.mult)
                    last.then_inc(scr_free[bank] if t else yn_s, 1)

            def store_out(section, b):
                ps, free = scratch(section, b, "OT'")
                if section == "tail":
                    dve.wait_ge(out_stored, 16 * (b - 1))
                dve.tensor_copy(o_sb[:, :], ps[:, 0:E]).then_inc(free, 1)

            def stage(section, b, name):
                c = b + 1
                if name == "ln1":
                    layer_stats(x_sb[:, :], x_in, 16 * (c + 1), st1[:, :], mv1[:, :], stats1, mean1, c + 1)
                    normalise(xhat[:, :], x_sb[:, :], mv1, rstd1, rstd1_s, c + 1, xhat_s)
                if name == "xT":
                    shift_in(section, c, "xT", xn, "ln1", prev1_s, sx, sx_s)
                    mix_in(c)
                if name in ("mix0", "mix1", "mix2"):
                    mixes(section, c, int(name[3]))
                if name == "vg":
                    bonus_rk(section, c)
                    make_gate(section, c)
                if name in ("vr0", "vr1", "vr2", "vr3"):
                    key_value(section, c, int(name[2]))
                if name in ("scan0", "scan1", "scan2", "scan3"):
                    scans(section, c, int(name[4]))
                if name == "red":
                    group_norm(section, c)
                if name == "hrstd":
                    group_normed(c)
                if name == "attT":
                    gated(section, c)
                if name == "wo":
                    residual1(section, c)
                if name == "xhat2":
                    residual1_normed(c)
                if name == "x2T":
                    ffn_in(section, c)
                if name == "kkrr":
                    ffn_mid(section, c)
                if name == "ffn":
                    make_z(section, c)
                if name.startswith("AT"):
                    attention_turned(section, b, name)
                if name == "Y'":
                    finish(section, b)
                    finish_normed(section, b)
                if name == "OT'":
                    store_out(section, b)

            def step(section, b):
                if section != "first":
                    turned(b - 1, NP - 1)
                for name in stages(section, 0, "start"):
                    stage(section, b, name)
                qk_out(b, 0)
                if section != "first":
                    attended(b - 1, NP - 2)
                for p in range(NP):
                    maxes(b, p, 0)
                    maxes(b, p, 1)
                    for name in stages(section, p, "a"):
                        stage(section, b, name)
                    if p < NP - 1:
                        qk_out(b, p + 1)
                    if p > 0:
                        turned(b, p - 1)
                    for name in stages(section, p, "b"):
                        stage(section, b, name)
                    if p > 1:
                        attended(b, p - 2)
                    elif p == 1 and section != "first":
                        attended(b - 1, NP - 1)
                    for name in stages(section, p, "c"):
                        stage(section, b, name)
                if section == "loop":
                    dve.wait_ge(out_stored, 16 * b)

            def tail():
                turned(B - 1, NP - 1)
                attended(B - 1, NP - 2)
                attention_turned("tail", B, "AT2'")
                attended(B - 1, NP - 1)
                attention_turned("tail", B, "AT3'")
                finish("tail", B)
                finish_normed("tail", B)
                store_out("tail", B)

            dve.wait_ge(in_cst, 32)
            dve.wait_ge(setup, SETUP_STEPS)
            dve.wait_ge(bias_scaled, 1)
            for name in ORDER:
                if included("prologue", name):
                    stage("prologue", -1, name)
            run_steps(dve, step, tail)

        @block.tensor
        def _(pe):
            def read(section, b, name):
                bank, _, before = use(section, name, b)
                pe.wait_ge(scr_free[bank], before + 1)

            def scratch(section, b, name):
                bank, _, before = use(section, name, b)
                if section != "prologue" or before > 0:
                    pe.wait_ge(scr_free[bank], before)
                return scr[bank]

            def tokens_first(ps, weight, src, col0=0):
                for t in range(ET):
                    last = pe.matmul(ps[:, col0:col0 + E], src[:, t, :], weight[:, t, :], start=(t == 0), stop=(t == ET - 1))
                return last

            def channels_first(ps, weight, src, col0=0):
                for f in range(ET):
                    for t in range(ET):
                        last = pe.matmul(ps[:, col0 + f * T:col0 + (f + 1) * T], weight[:, t, f * P:(f + 1) * P],
                                         src[:, t, :], start=(t == 0), stop=(t == ET - 1))
                return last

            def turn(ps, src):
                for t in range(ET):
                    last = pe.transpose(ps[:, t * T:(t + 1) * T], src[:, t * P:(t + 1) * P], ident[:, :])
                return last

            def l0_use(section, c, name):
                b = c - 1
                if name == "xT":
                    pe.wait_ge(xhat_s, c + 1)
                    last = turn(scratch(section, b, name), xhat)
                elif name == "mixin":
                    pe.wait_ge(xin_s, c + 1)
                    ps = scratch(section, b, name)
                    for t in range(ET):
                        pe.matmul(ps[:, 0:T], w1_sb[:, t, 0:4 * XM], xin[:, t, :], start=(t == 0), stop=(t == ET - 1))
                    for t in range(ET):
                        last = pe.matmul(ps[0:XM, T:2 * T], w1_sb[:, t, 4 * XM:5 * XM], xin[:, t, :],
                                         start=(t == 0), stop=(t == ET - 1))
                elif name in ("mix0", "mix1", "mix2"):
                    if name == "mix0":
                        read(section, b, "mixin")
                    slots = MIX_USES[int(name[3])][1]
                    ps = scratch(section, b, name)
                    for k, slot in enumerate(slots):
                        m = MIX_ORDER[slot]
                        for t in range(ET):
                            w = w2a_sb[:, m, t * P:(t + 1) * P] if m < 4 else w2b_sb[:, t * P:(t + 1) * P]
                            v = xxx[:, :] if m < 4 else xxx4[:, :]
                            last = pe.matmul(ps[:, (k * ET + t) * T:(k * ET + t + 1) * T], w, v, start=True, stop=True)
                elif name == "dec1":
                    pe.wait_ge(x5_s, 3 * c + 1)
                    ps = scratch(section, b, name)
                    for t in range(ET):
                        last = pe.matmul(ps[0:XD, 0:T], dw1_sb[:, t, :], x5[:, SLOT_W, t, :], start=(t == 0), stop=(t == ET - 1))
                elif name == "dec2":
                    read(section, b, "dec1")
                    ps = scratch(section, b, name)
                    for t in range(ET):
                        last = pe.matmul(ps[:, t * T:(t + 1) * T], dw2_sb[:, t * P:(t + 1) * P], dtanh[:, :],
                                         start=True, stop=True)
                elif name == "kr":
                    pe.wait_ge(x5_s, 3 * c + 2)
                    ps = scratch(section, b, name)
                    channels_first(ps, l0_weight("Wk"), x5[:, SLOT_K])
                    last = channels_first(ps, l0_weight("Wr"), x5[:, SLOT_R], E)
                elif name == "vg":
                    pe.wait_ge(x5_s, 3 * c + 3)
                    ps = scratch(section, b, name)
                    tokens_first(ps, l0_weight("Wv"), x5[:, SLOT_V])
                    last = channels_first(ps, l0_weight("Wg"), x5[:, SLOT_G], E)
                elif name in ("vr0", "vr1", "vr2", "vr3"):
                    n = int(name[2])
                    pe.wait_ge(vrep_s, 4 * c + n + 1)
                    ps = scratch(section, b, name)
                    for d in range(4):
                        last = pe.transpose(ps[:, d * T:(d + 1) * T], vrep[:, n, d, :], ident[:, :])
                elif name == "red":
                    ps = scratch(section, b, name)
                    pe.wait_ge(bonus_s, c + 1)
                    for t in range(ET):
                        pe.matmul(ps[:, E + t * HT:E + (t + 1) * HT], bonus[:, t, :], head_ones[:, :], start=True, stop=True)
                    for n in range(4):
                        pe.wait_ge(rs_s, 4 * c + n + 1)
                        t, dh = n // 2, n % 2
                        for d in range(dh * 4, dh * 4 + 4):
                            last = pe.matmul(ps[:, t * P:(t + 1) * P], kv[:, t, d, :], select[:, d, :, :],
                                             start=(d == 0), stop=(d == SD - 1))
                elif name == "attT":
                    pe.wait_ge(yhat_s, c + 1)
                    last = turn(scratch(section, b, name), yhat)
                elif name == "wo":
                    pe.wait_ge(ygT_s, c + 1)
                    last = tokens_first(scratch(section, b, name), l0_weight("Wo"), ygT)
                elif name == "x2T":
                    pe.wait_ge(xhat2_s, c + 1)
                    last = turn(scratch(section, b, name), xhat2)
                elif name == "kkrr":
                    pe.wait_ge(xkr_s, c + 1)
                    ps = scratch(section, b, name)
                    channels_first(ps, l0_weight("fWk"), xk)
                    last = tokens_first(ps, l0_weight("fWr"), xr, E)
                else:
                    assert name == "ffn", name
                    pe.wait_ge(ksq_s, c + 1)
                    last = tokens_first(scratch(section, b, name), l0_weight("fWv"), ksq)
                last.then_inc(scr_ready, 1)

            def project(b, p):
                n = NP * b + p
                if p == 0:
                    pe.wait_ge(z_s, b + 1)
                    pe.wait_ge(u_s, b + 1)
                if not (isinstance(b, int) and n == 0):
                    pe.wait_ge(qk_s, 2 * n)
                for a in range(2):
                    for lt in range(ET):
                        dst = qk_ps[:, a, lt * P:(lt + 1) * P]
                        o = slice(a * HD + p * P, a * HD + (p + 1) * P)
                        pe.matmul(dst, wqkv_sb[:, lt, o], z_sb[:, lt * P:(lt + 1) * P], start=True, stop=False)
                        last = pe.matmul(dst, winj_sb[:, lt, o], u_sb[:, lt * P:(lt + 1) * P], start=False, stop=True)
                last.then_inc(proj_s, 1)

            def values(section, b, name):
                oh, lt = int(name[1]), int(name[2])
                ps = scratch(section, b, name)
                o = slice(2 * HD + oh * (HD // 2), 2 * HD + (oh + 1) * (HD // 2))
                pe.matmul(ps[:, :], z_sb[:, lt * P:(lt + 1) * P], wqkv_sb[:, lt, o], start=True, stop=False)
                pe.matmul(ps[:, :], u_sb[:, lt * P:(lt + 1) * P], winj_sb[:, lt, o], start=False, stop=True).then_inc(scr_ready, 1)

            def scores(section, b, p):
                pe.wait_ge(qk_s, 2 * (NP * b + p + 1))
                for h in range(2):
                    if p > 0 or section != "first":
                        pe.wait_ge(prob_s, 16 * b + (2 * p + h - 1))
                    rows = slice(h * DH, (h + 1) * DH)
                    for it in range(ET):
                        last = pe.matmul(s_ps[h][:, it, :], q_sb[rows, p % 2, it * P:(it + 1) * P], k_sb[rows, p % 2, :],
                                         start=True, stop=True)
                    last.then_inc(score_s, 1)

            def turn_probs(first, b, p):
                for h in range(2):
                    pe.wait_ge(prob_s, 16 * b + (2 * p + h + 1))
                    if not first:
                        pe.wait_ge(probT_s[h], NP * b + p)
                    for it in range(ET):
                        for jt in range(ET):
                            last = pe.transpose(t_ps[h][:, jt, it, :], prob[:, p % 2, h, it, jt * P:(jt + 1) * P], ident[:, :])
                    last.then_inc(turn_s, 1)

            def attend(first, b, p):
                if not first:
                    pe.wait_ge(attn_s, NP * b + p)
                for h in range(2):
                    pe.wait_ge(probT_s[h], NP * b + p + 1)
                    for it in range(ET):
                        for jt in range(ET):
                            last = pe.matmul(o_ps[:, h, it, 0:VW], probT[:, p % 2, h, jt, it, :], v1_sb[:, jt, 2 * p + h, :],
                                             start=(jt == 0), stop=(jt == ET - 1))
                last.then_inc(pv_s, 1)

            def turn_attn(section, b, name, entry):
                k = int(name[2])
                pe.wait_ge(attn_s, NP * entry + (2 * k + 2))
                ps = scratch(section, b, name)
                for a in range(2):
                    for it in range(ET):
                        last = pe.transpose(ps[:, (a * ET + it) * P:(a * ET + it + 1) * P],
                                            attn[:, it, (2 * k + a) * P:(2 * k + a + 1) * P], ident[:, :])
                last.then_inc(scr_ready, 1)

            def output(section, b):
                read(section, b, "AT3'")
                read(section, b, "AT2'")
                pe.wait_ge(zres_s, b)
                ps = scratch(section, b, "Y'")
                for lt in range(ET):
                    dst = ps[:, lt * P:(lt + 1) * P]
                    for p in range(NP):
                        pe.matmul(dst, attnT[:, p, lt * P:(lt + 1) * P], wo1_sb[:, p, :], start=(p == 0), stop=False)
                    last = pe.matmul(dst, zres[:, lt * P:(lt + 1) * P], ident[:, :], start=False, stop=True)
                last.then_inc(scr_ready, 1)

            def output_turned(section, b):
                read(section, b, "Y'")
                ps = scratch(section, b, "OT'")
                for t in range(ET):
                    last = pe.transpose(ps[:, t * P:(t + 1) * P], yn[:, t, :], ident[:, :])
                last.then_inc(scr_ready, 1)

            def stage(section, b, name):
                if name in NO_SCRATCH:
                    return
                if name.startswith("V"):
                    values(section, b, name)
                elif name.startswith("AT"):
                    turn_attn(section, b, name, b - 1 if name.endswith("'") else b)
                elif name == "Y'":
                    output(section, b)
                elif name == "OT'":
                    output_turned(section, b)
                else:
                    l0_use(section, b + 1, name)

            def step(section, b):
                if section != "first":
                    turn_probs(False, b - 1, NP - 1)
                project(b, 0)
                if section != "first":
                    attend(False, b - 1, NP - 2)
                for p in range(NP):
                    scores(section, b, p)
                    for name in stages(section, p, "a"):
                        stage(section, b, name)
                    if p < NP - 1:
                        project(b, p + 1)
                    if p > 0:
                        turn_probs(section == "first" and p == 1, b, p - 1)
                    for name in stages(section, p, "b"):
                        stage(section, b, name)
                    if p > 1:
                        attend_values(section, b, p - 2)
                        attend(section == "first" and p == 2, b, p - 2)
                    elif p == 1 and section != "first":
                        attend(False, b - 1, NP - 1)
                    for name in stages(section, p, "c"):
                        stage(section, b, name)
            def attend_values(section, b, p):
                if p in (0, 4):
                    read(section, b, f"V{p // 4}0")
                    read(section, b, f"V{p // 4}1")

            def tail():
                turn_probs(False, B - 1, NP - 1)
                attend(False, B - 1, NP - 2)
                turn_attn("tail", B, "AT2'", B - 1)
                attend(False, B - 1, NP - 1)
                turn_attn("tail", B, "AT3'", B - 1)
                output("tail", B)
                output_turned("tail", B)

            pe.wait_ge(setup, SETUP_STEPS)
            pe.wait_ge(in_l0a, 16 * 9)
            for name in L0_USES:
                if name == "wo":
                    pe.wait_ge(in_l0b, 16)
                stage("prologue", -1, name)
            pe.wait_ge(in_l1a, 32)
            pe.wait_ge(in_l1b, 16)
            run_steps(pe, step, tail)
    return nc


def kernel(**inputs):
    import numpy as np
    import concourse.bacc as bacc
    from concourse.bass_utils import run_bass_kernel_spmd

    a = {k: np.asarray(v) for k, v in inputs.items()}
    l0 = {k[len("L0_xattn_"):]: v for k, v in a.items() if k.startswith("L0_xattn_")}
    l1 = {k[len("L1_xattn_"):]: v for k, v in a.items() if k.startswith("L1_xattn_")}

    def tiles(v):
        v = v.reshape(-1, ET, P)
        return np.moveaxis(v, 2, 0).reshape(P, -1)

    def rows(w):
        return np.moveaxis(w.reshape(ET, P, -1), 1, 0)

    parts = {
        "ln1_w": l0["ln1_w"], "ln1_b": l0["ln1_b"], "ln2_w": l0["ln2_w"], "ln2_b": l0["ln2_b"],
        "maa_x": l0["maa_x"], "maa": l0["maa_stack"], "decay": l0["time_decay"], "bonus": l0["faaaa"].reshape(E),
        "gn_w": l0["gn_w"], "gn_b": l0["gn_b"], "ffn_k": l0["ffn_maa_k"], "ffn_r": l0["ffn_maa_r"],
    }
    laid = {k: tiles(v) for k, v in parts.items()}
    laid["bo"] = l1["bo"].reshape(P, 1)
    laid["q_bias"] = l1["r_w_bias"].reshape(NP, P).T
    ctx_np = a["ctx_2048"]
    laid["prev"] = tiles(np.stack([ctx_np[:, 1, :], ctx_np[:, 0, :]]))
    arrays = {
        "x": a["x"],
        "ctx_in": ctx_np,
        "consts": np.concatenate([laid[name] for name, _ in CONSTS], axis=1),
        "state0": np.moveaxis(ctx_np[:, 2:2 + SD, :].reshape(B, ET, P, SD), 2, 0),
        "l0w": np.stack([rows(l0[n].T) for n in
                         ("Wk", "Wr", "Wv", "Wg", "Wo", "ffn_Wk", "ffn_Wr", "ffn_Wv")], axis=1),
        "maa_w1": rows(l0["maa_w1"]),
        "maa_w2": l0["maa_w2"].reshape(MIX * XM, E),
        "decay_w1": rows(l0["decay_w1"]),
        "decay_w2": l0["decay_w2"],
        "wqkv": np.stack([l1["Wqkv0"].T, l1["Wqkv1"].T], axis=1),
        "winj": np.stack([l1["Winj0"].T, l1["Winj1"].T], axis=1),
        "wo1": np.moveaxis(l1["Wo"].T.reshape(NP, P, P), 1, 0),
    }
    arrays = {f"in_{k}": np.ascontiguousarray(v) for k, v in arrays.items()}
    nc = bacc.Bacc("TRN2", target_bir_lowering=False, num_devices=1)
    args = [nc.dram_tensor(k, v.shape, mybir.dt.from_np(v.dtype), kind="ExternalInput").ap() for k, v in arrays.items()]
    args.append(nc.dram_tensor("out_z", (B, T, E), F32, kind="ExternalOutput").ap())
    rwkv_then_attention(nc, *args)
    r = run_bass_kernel_spmd(nc, [arrays], core_ids=[0])
    return r.results[0]["out_z"]
```

```python
from contextlib import ExitStack

import concourse.bass as bass
from concourse import mybir

F32 = mybir.dt.float32
F32R = mybir.dt.float32r
ALU = mybir.AluOpType
ACT = mybir.ActivationFunctionType
AX = mybir.AxisListType

P = 128
B = 8
T = 128
E = 256
ET = E // P
SD = 8
HT = P // SD
H0 = E // SD
MIX = 5
XM = 32
XD = 64
EPS = 1e-5
NH = 16
DH = 64
NP = NH // 2
HD = NH * DH
SCALE = DH ** -0.5

MIX_ORDER = [1, 0, 2, 3, 4]
SLOT_W, SLOT_K, SLOT_V, SLOT_R, SLOT_G = range(MIX)
MIX_USES = [("mix0", [0, 1]), ("mix1", [2, 3]), ("mix2", [4])]

CONSTS = [("ln1_w", ET), ("ln1_b", ET), ("ln2_w", ET), ("ln2_b", ET), ("maa_x", ET), ("maa", MIX * ET),
          ("decay", ET), ("bonus", ET), ("gn_w", ET), ("gn_b", ET), ("ffn_k", ET), ("ffn_r", ET),
          ("q_bias", NP), ("bo", 1), ("prev", 2 * B * ET)]
COL, _n = {}, 0
for _name, _w in CONSTS:
    COL[_name] = _n
    _n += _w
NCONST = _n

L0W = ["Wk", "Wr", "Wv", "Wg", "Wo", "fWk", "fWr", "fWv"]

SCHEDULE = {
    (0, "start"): ["ln1", "xhat", "xT"], (0, "a"): ["mixin"], (0, "b"): ["mix0", "split"],
    (1, "a"): ["mix1", "mix2"], (1, "b"): ["V00"], (1, "c"): ["V01", "dec1"],
    (2, "a"): ["Y'"], (2, "b"): ["dec2", "kr", "vg"], (2, "c"): ["vr0"],
    (3, "a"): ["scan0", "vr1"], (3, "c"): ["vr2", "YT'"],
    (4, "a"): ["scan1", "scan2", "yst'"], (4, "b"): ["vr3", "scan3", "red0"], (4, "c"): ["yn'", "red1", "V10"],
    (5, "a"): ["hrstd0", "hrstd1"], (5, "b"): ["V11"], (5, "c"): ["attT"],
    (6, "a"): ["wo", "xhat2"], (6, "c"): ["x2T"],
    (7, "a"): ["OT'", "kkrr"], (7, "c"): ["ffn"],
}
ORDER = [name for p in range(NP) for phase in ("start", "a", "b", "c")
         for name in SCHEDULE.get((p, phase), [])]
L1_STAGES = ["split", "V00", "V01", "V10", "V11", "Y'", "YT'", "yst'", "yn'", "OT'"]
NO_SCRATCH = ["yst'", "yn'", "split", "ln1", "xhat", "scan0", "scan1", "scan2", "scan3", "hrstd0", "hrstd1", "xhat2"]

STEP_USES = [name for name in ORDER if name not in NO_SCRATCH]
L0_USES = [name for name in STEP_USES if name not in L1_STAGES]
FILL = {
    "xT": 9, "mixin": 10, "mix0": 5, "dec1": 4, "dec2": 3, "vr0": 4, "vr1": 2, "vr2": 3,
    "red0": 1, "red1": 4, "attT": 29, "wo": 7, "x2T": 12, "kkrr": 13, "ffn": 5,
}
SECTIONS = {
    "prologue": list(L0_USES),
    "first": [u for u in STEP_USES if not u.endswith("'")],
    "loop": list(STEP_USES),
    "last": [u for u in STEP_USES if u not in L0_USES],
    "tail": ["Y'", "YT'", "OT'"],
}
LOOP_STEPS = B - 2
START_STEPS = 5
SETUP_STEPS = START_STEPS + 8


def scratch_plan():
    plan, total, of_bank = {}, 0, [0, 0]
    for section, uses in SECTIONS.items():
        times = LOOP_STEPS if section == "loop" else 1
        steps = (len(uses), [len(uses[n::2]) for n in range(2)])
        for n, name in enumerate(uses):
            bank = n % 2
            plan[section, name] = (bank, total + n, of_bank[bank] + n // 2,
                                   steps[0] if section == "loop" else 0,
                                   steps[1][bank] if section == "loop" else 0)
        total += times * steps[0]
        of_bank = [of_bank[n] + times * steps[1][n] for n in range(2)]
    return plan


def rwkv_then_attention(nc, x, ctx_in, consts, state0, l0w, maa_w1, maa_w2, decay_w1, decay_w2,
                        wqkv, winj, wo1, out):
    plan = scratch_plan()
    with ExitStack() as stack:
        def sb(name, shape, dt=F32):
            return stack.enter_context(nc.sbuf_tensor(name, shape, dt))

        def psum(name, shape, dt=F32):
            return stack.enter_context(nc.psum_tensor(name, shape, dt))

        def sem(name):
            return stack.enter_context(nc.semaphore(name))

        cst = sb("cst", [P, NCONST])
        s0_all = sb("s0_all", [P, B, ET, SD])
        l0w_sb = sb("l0w_sb", [P, len(L0W), ET, E])
        w1_sb = sb("w1_sb", [P, ET, MIX * XM])
        w2a_sb = sb("w2a_sb", [P, 4, E])
        w2b_sb = sb("w2b_sb", [XM, E])
        dw1_sb = sb("dw1_sb", [P, ET, XD])
        dw2_sb = sb("dw2_sb", [XD, E])
        wqk_sb = sb("wqk_sb", [P, 2, 2, 2 * HD])
        wv_hi = sb("wv_hi", [P, 2, 2, HD], F32R)
        wv_lo = sb("wv_lo", [P, 2, 2, HD], F32R)
        wo1_sb = sb("wo1_sb", [P, NP, P])
        ident = sb("ident", [P, P])
        head_ones = sb("head_ones", [P, HT])
        select = sb("select", [P, HT, 2 * SD])
        minus_half = sb("minus_half", [P, HT])
        one = sb("one", [P, 1])
        eps_row = sb("eps_row", [P, ET])
        carrier = sb("carrier", [P, 2])
        warm = sb("warm", [P, 1])

        x_sb = sb("x_sb", [P, E])
        st1 = sb("st1", [P, 6])
        mv1 = sb("mv1", [P, 2])
        ve1 = sb("ve1", [P, 1])
        rstd1 = sb("rstd1", [P, 1])
        xhat = sb("xhat", [P, E])
        xn = sb("xn", [P, ET, T + 1])
        sx = sb("sx", [P, ET, T])
        bonus = sx
        xn2, sx2 = xn, sx
        xxx = sb("xxx", [P, T])
        dtanh = xxx[0:XD, :]
        xxx4 = sb("xxx4", [XM, T])
        x5 = sb("x5", [P, MIX, ET, T])
        w_sb = sb("w_sb", [P, ET, T])
        kr_sb = sb("kr_sb", [P, 2, ET, T])
        v_sb = sb("v_sb", [P, E])
        vrep = sb("vrep", [P, 4, 4, P])
        kv = vrep
        g_sb = sb("g_sb", [P, ET, T])
        gate = sb("gate", [P, ET, T])
        states = sb("states", [P, ET, SD, T + 1])
        bonus_v = sb("bonus_v", [P, E])
        att = sb("att", [P, E])
        hsum = sb("hsum", [P, ET, HT])
        hsq = sb("hsq", [P, ET, HT])
        hve = sb("hve", [P, ET, HT])
        hrstd = sb("hrstd", [P, ET, HT])
        x1 = sb("x1", [P, E])
        st2 = sb("st2", [P, 6])
        mv2 = sb("mv2", [P, 2])
        ve2 = sb("ve2", [P, 1])
        rstd2 = sb("rstd2", [P, 1])
        yT, ygT, xk, xr = (x5[:, n, :, :] for n in range(4))
        ksq = sb("ksq", [P, ET, T])
        xin = ksq
        rtanh = sb("rtanh", [P, E])

        z_sb = sb("z_sb", [P, E])
        zres = sb("zres", [P, E])
        u_in = sb("u_in", [P, E])
        u_sb = sb("u_sb", [P, E])
        zu_hi = sb("zu_hi", [P, 2, E], F32R)
        zu_lo = sb("zu_lo", [P, 2, E], F32R)
        q_hi = sb("q_hi", [P, 2, E], F32R)
        q_lo = sb("q_lo", [P, 2, E], F32R)
        k_hi = sb("k_hi", [P, 2, E], F32R)
        k_lo = sb("k_lo", [P, 2, E], F32R)
        v_hi = sb("v_hi", [P, ET, NP, 3 * DH], F32R)
        v_lo = sb("v_lo", [P, ET, NP, 3 * DH], F32R)
        nmax = sb("nmax", [P, 2, 2, ET])
        prob = sb("prob", [P, 2, 2, ET, E])
        probT_hi = sb("probT_hi", [P, 2, 2, ET, E], F32R)
        probT_lo = sb("probT_lo", [P, 2, 2, ET, E], F32R)
        wv_in = [prob[:, :, :, :, :].rearrange("p a h i j -> p a (h i j)"),
                 vrep[:, :, :, :].rearrange("p n d x -> p (n d x)")]
        prob_sum = sb("prob_sum", [P, 2, 2, ET])
        rden = sb("rden", [P, 2, 2, ET])
        attnT = sb("attnT", [P, NP, E])
        y_sb = sb("y_sb", [P, E])
        yn = y_sb[:, :].rearrange("p (t n) -> p t n", t=ET)
        st3 = sb("st3", [P, ET, 6])
        mv3 = sb("mv3", [P, ET, 2])
        ve3 = sb("ve3", [P, ET])
        rstd3 = sb("rstd3", [P, ET])
        o_sb = sb("o_sb", [P, E])

        qk_ps = psum("qk_ps", [P, 2, E])
        s_ps = [psum(f"s_ps{h}", [P, ET, E]) for h in range(2)]
        t_ps = [psum(f"t_ps{h}", [P, ET, E]) for h in range(2)]
        o_ps = psum("o_ps", [P, E])
        scr = [psum(f"scr{n}", [P, 512]) for n in range(2)]

        x_in, u_loaded, out_stored = sem("x_in"), sem("u_loaded"), sem("out_stored")
        in_cst, in_state, in_mix, in_l0a, in_l0b = (
            sem(f"in_{n}") for n in ("cst", "state", "mix", "l0a", "l0b"))
        in_l1a, in_wv0, in_wv1, in_wo1 = (sem(f"in_{n}") for n in ("l1a", "wv0", "wv1", "wo1"))
        setup = sem("setup")
        w2a_zeroed = sem("w2a_zeroed")
        wv_hi_s, wv_lo_s = sem("wv_hi_s"), sem("wv_lo_s")
        scr_ready = sem("scr_ready")
        scr_free = [sem(f"scr_free{n}") for n in range(2)]
        stats1, mean1, eps1, rstd1_s, xhat_s = (sem(n) for n in ("stats1", "mean1", "eps1", "rstd1_s", "xhat_s"))
        prev1_s, sx_s, xin_s = (sem(n) for n in ("prev1_s", "sx_s", "xin_s"))
        x5_s = sem("x5_s")
        w_s, bonus_s, gate_s = sem("w_s"), sem("bonus_s"), sem("gate_s")
        s0_s = sem("s0_s")
        v_hi_s = sem("v_hi_s")
        v_s = sem("v_s")
        vrep_s = sem("vrep_s")
        scan_s = sem("scan_s")
        rs_s = sem("rs_s")
        gn_s = sem("gn_s")
        hrstd_s, yhat_s, ygT_s = (sem(n) for n in ("hrstd_s", "yhat_s", "ygT_s"))
        stats2, mean2, eps2, rstd2_s, xhat2_s = (sem(n) for n in ("stats2", "mean2", "eps2", "rstd2_s", "xhat2_s"))
        prev2_s, sx2_s, xkr_s = (sem(n) for n in ("prev2_s", "sx2_s", "xkr_s"))
        relu_s, ksq_s, z_s, zres_s, u_s = (sem(n) for n in ("relu_s", "ksq_s", "z_s", "zres_s", "u_s"))
        proj_s = sem("proj_s")
        qk_hi_s = sem("qk_hi_s")
        qk_s = sem("qk_s")
        zu_hi_s, zu_lo_s = sem("zu_hi_s"), sem("zu_lo_s")
        score_s = sem("score_s")
        max_s = sem("max_s")
        prob_s = sem("prob_s")
        norm_s = sem("norm_s")
        turn_s = sem("turn_s")
        probT_hi_s, probT_s = sem("probT_hi_s"), sem("probT_s")
        pv_s = sem("pv_s")
        rden_s = sem("rden_s")
        attn_s = sem("attn_s")
        y_s = sem("y_s")
        stats3, mean3, eps3, rstd3_s, yn_s = (sem(n) for n in ("stats3", "mean3", "eps3", "rstd3_s", "yn_s"))

        block = stack.enter_context(nc.Block())

        def col(name, n=0):
            return cst[:, COL[name] + n:COL[name] + n + 1]

        def l0_weight(name):
            return l0w_sb[:, L0W.index(name), :, :]

        def use(section, name, b):
            bank, before, bank_before, step, bank_step = plan[section, name]
            if section != "loop":
                return bank, before + 1, bank_before
            return bank, b * step + (before + 1 - step), b * bank_step + (bank_before - bank_step)

        def included(section, name):
            if name in L1_STAGES:
                return section in ("loop", "last") or (section == "first" and not name.endswith("'")) or (
                    section == "tail" and name.endswith("'"))
            return section in ("prologue", "first", "loop")

        def stages(section, slot, phase):
            return [name for name in SCHEDULE.get((slot, phase), []) if included(section, name)]

        def pair_values(v, oh, lt):
            return v[:, lt, 4 * oh:4 * oh + 4, :].rearrange("p n (b d) -> p n b d", b=3)[:, :, 0:3:2, :]

        def spread_v(n):
            t, dh = n // 2, n % 2
            src = v_sb[:, t * P:(t + 1) * P].rearrange("p (h d) -> p d h", d=SD)[:, dh * 4:dh * 4 + 4, :]
            dst = vrep[:, n, :, :].rearrange("p d (h k) -> p d h k", k=SD)
            return dst, src[:, :, :, None].to_broadcast([P, 4, HT, SD])

        def run_steps(eng, step, tail=None):
            step("first", 0)
            with eng.Fori(1, B - 1) as b:
                step("loop", b)
            step("last", B - 1)
            if tail:
                tail()

        @block.sync
        def _(sp):
            sp.dma_start(x_sb[:, :], x[0]).then_inc(x_in, 16)
            sp.dma_start(cst[:, :], consts).then_inc(in_cst, 16)
            sp.dma_start(w1_sb[:, :, :], maa_w1).then_inc(in_mix, 16)
            sp.wait_ge(w2a_zeroed, 1)
            for m in range(4):
                rows = slice(m * XM, (m + 1) * XM)
                sp.dma_start(w2a_sb[rows, m, :], maa_w2[rows, :]).then_inc(in_mix, 16)
            sp.dma_start(w2b_sb[:, :], maa_w2[4 * XM:5 * XM, :]).then_inc(in_mix, 16)
            sp.dma_start(dw1_sb[:, :, :], decay_w1).then_inc(in_l0a, 16)
            sp.dma_start(dw2_sb[:, :], decay_w2).then_inc(in_l0a, 16)
            sp.dma_start(s0_all[:, :, :, :], state0).then_inc(in_state, 16)
            sp.dma_start(l0w_sb[:, 0:4, :, :], l0w[:, 0:4]).then_inc(in_l0a, 16)
            sp.dma_start(l0w_sb[:, 4:8, :, :], l0w[:, 4:8]).then_inc(in_l0b, 16)
            sp.dma_start(u_in[:, :], ctx_in[0]).then_inc(u_loaded, 16)
            for n, w in enumerate((wqkv, winj)):
                sp.dma_start(wqk_sb[:, n, :, :], w[:, :, 0:2 * HD]).then_inc(in_l1a, 16)
            sp.dma_start(wo1_sb[:, :, :], wo1).then_inc(in_wo1, 16)
            sp.dma_start(wv_in[0], wqkv[:, :, 2 * HD:3 * HD]).then_inc(in_wv0, 16)
            sp.wait_ge(scr_ready, use("prologue", "red1", -1)[1])
            sp.dma_start(wv_in[1], winj[:, :, 2 * HD:3 * HD]).then_inc(in_wv1, 16)

            def load_next(section, b):
                bank, _, before = use(section, "wo", b - 1)
                sp.wait_ge(scr_free[bank], before + 1)
                sp.dma_start(x_sb[:, :], x[b + 1]).then_inc(x_in, 16)
                sp.wait_ge(u_s, b + 1)
                sp.dma_start(u_in[:, :], ctx_in[b + 1]).then_inc(u_loaded, 16)

            def store(section, b):
                bank, _, before = use(section, "OT'", b + 1)
                sp.wait_ge(scr_free[bank], before + 1)
                sp.dma_start(out[b], o_sb[:, :]).then_inc(out_stored, 16)

            load_next("prologue", 0)
            load_next("first", 1)
            with sp.Fori(1, B - 2) as b:
                store("loop", b - 1)
                load_next("loop", b + 1)
            store("loop", B - 3)
            store("last", B - 2)
            store("tail", B - 1)
            sp.wait_ge(out_stored, 16 * B)

        @block.gpsimd
        def _(pool):
            done = 0

            def chained(ins):
                nonlocal done
                done += 1
                ins.then_inc(setup, 1)
                pool.wait_ge(setup, done)

            def copy(dst, src, shape):
                ones = one[:, :]
                while len(ones.shape) < len(shape):
                    ones = ones[:, None]
                return pool.tensor_tensor(dst, src, ones.to_broadcast(shape), ALU.mult)

            def rsqrt(var, ve, rstd, n, wait_var, eps_sem, rstd_sem, val):
                pool.wait_ge(wait_var, val)
                pool.tensor_tensor(ve, var, eps_row[:, 0:n], ALU.add).then_inc(eps_sem, 1)
                pool.wait_ge(eps_sem, val)
                pool.tensor_tensor(rstd, ve, minus_half[:, 0:n], ALU.pow).then_inc(rstd_sem, 1)

            def shifted_rows(c):
                n = COL["prev"]
                prev = cst[:, n:n + 2 * B * ET].rearrange("p (r b t) -> p r b t", r=2, b=B)
                pool.tensor_copy(xn[:, :, 0:1], prev[:, 0, bass.ds(c, 1), :].rearrange("p b t -> p t b"))\
                    .then_inc(prev1_s, 1)

            def shifted_row2(c):
                n = COL["prev"]
                prev = cst[:, n:n + 2 * B * ET].rearrange("p (r b t) -> p r b t", r=2, b=B)
                pool.tensor_copy(xn2[:, :, 0:1], prev[:, 1, bass.ds(c, 1), :].rearrange("p b t -> p t b"))\
                    .then_inc(prev2_s, 1)

            def first_states(c):
                pool.tensor_copy(states[:, :, :, 0:1],
                                 s0_all[:, bass.ds(c, 1), :, :].rearrange("p b t d -> p t d b")).then_inc(s0_s, 1)

            def mix_add(section, c, n):
                name, slots = MIX_USES[n]
                bank, _, before = use(section, name, c - 1)
                pool.wait_ge(scr_free[bank], before + 1)
                a, z = slots[0], slots[-1] + 1
                xb = xn[:, None, :, 1:T + 1].to_broadcast([P, z - a, ET, T])
                pool.tensor_tensor(x5[:, a:z, :, :], x5[:, a:z, :, :], xb, ALU.add).then_inc(x5_s, 1)

            def receive(c, n):
                t, dh = n // 2, n % 2
                d = slice(dh * 4, dh * 4 + 4)
                pool.wait_ge(scan_s, 4 * c + n + 1)
                r = kr_sb[:, 1, t:t + 1, :].to_broadcast([P, 4, T])
                pool.tensor_tensor(kv[:, n, :, :], states[:, t, d, 0:T], r, ALU.mult).then_inc(rs_s, 1)

            def stage(section, b, name):
                c = b + 1
                if name == "ln1":
                    rsqrt(mv1[:, 1:2], ve1[:, :], rstd1[:, :], 1, mean1, eps1, rstd1_s, c + 1)
                    shifted_rows(c)
                if name in ("mix0", "mix1", "mix2"):
                    mix_add(section, c, int(name[3]))
                if name == "vg":
                    if section == "prologue":
                        pool.wait_ge(in_state, 16)
                    first_states(c)
                    shifted_row2(c)
                if name in ("scan0", "scan1", "scan2", "scan3"):
                    receive(c, int(name[4]))
                if name in ("red0", "red1"):
                    t = int(name[3])
                    pool.wait_ge(gn_s, 14 * c + 7 * t + 7)
                    pool.tensor_tensor(hrstd[:, t, :], hve[:, t, :], minus_half[:, :], ALU.pow).then_inc(hrstd_s, 1)
                if name == "wo":
                    rsqrt(mv2[:, 1:2], ve2[:, :], rstd2[:, :], 1, mean2, eps2, rstd2_s, c + 1)
                if name == "split":
                    pool.wait_ge(zu_hi_s, b + 1)
                    for n, src in enumerate((z_sb, u_sb)):
                        last = pool.tensor_tensor(zu_lo[:, n, :], src[:, :], zu_hi[:, n, :], ALU.subtract)
                    last.then_inc(zu_lo_s, 1)
                if name == "yst'":
                    rsqrt(mv3[:, :, 1], ve3[:, :], rstd3[:, :], ET, mean3, eps3, rstd3_s, b)

            def normalise(b, p):
                pool.wait_ge(rden_s, NP * b + (p + 1))
                for h in range(2):
                    x = prob[:, p % 2, h, :, :]
                    r = rden[:, p % 2, h, :].rearrange("p (i o) -> p i o", o=1).to_broadcast([P, ET, E])
                    pool.tensor_tensor(x, x, r, ALU.mult).then_inc(norm_s, 1)

            def keep_z(section, b):
                if section != "first":
                    pool.wait_ge(y_s, b)
                pool.wait_ge(z_s, b + 1)
                pool.tensor_tensor(zres[:, :], z_sb[:, :], col("bo").to_broadcast([P, E]), ALU.add).then_inc(zres_s, 1)

            def take_u(b):
                pool.wait_ge(proj_s, NP * b)
                pool.wait_ge(u_loaded, 16 * (b + 1))
                copy(u_sb[:, :], u_in[:, :], [P, E]).then_inc(u_s, 1)

            def step(section, b):
                if included(section, "ln1"):
                    stage(section, b, "ln1")
                for p in range(NP):
                    for name in stages(section, p, "a"):
                        stage(section, b, name)
                    normalise(b, p)
                    for name in stages(section, p, "b"):
                        stage(section, b, name)
                    for name in stages(section, p, "c"):
                        stage(section, b, name)
                    if p == 4:
                        keep_z(section, b)
                    if p == 6 and section != "last":
                        take_u(b + 1)

            chained(pool.memset(carrier[:, :], 0.0))
            chained(pool.memset(minus_half[:, :], -0.5))
            chained(pool.memset(eps_row[:, :], EPS))
            chained(pool.memset(ident[:, :], 0.0))
            chained(pool.affine_select(out=ident[:, :], in_=ident[:, :], compare_op=ALU.not_equal, fill=1.0,
                                       base=0, pattern=[[-1, P]], channel_multiplier=1))
            assert done == START_STEPS
            pool.wait_ge(in_cst, 16)
            stage("prologue", -1, "ln1")
            chained(pool.memset(head_ones[:, :], 1.0))
            chained(pool.affine_select(out=head_ones[:, :], in_=head_ones[:, :], compare_op=ALU.is_ge, fill=0.0,
                                       base=0, pattern=[[-SD, HT]], channel_multiplier=1))
            chained(pool.affine_select(out=head_ones[:, :], in_=head_ones[:, :], compare_op=ALU.is_ge, fill=0.0,
                                       base=SD - 1, pattern=[[SD, HT]], channel_multiplier=-1))
            chained(pool.memset(select[:, :, :], 0.0))
            chained(pool.tensor_copy(select[:, :, SD], head_ones[:, :]))
            chained(pool.memset(one[:, :], 1.0))
            chained(pool.memset(v_hi[:, :, :, DH:2 * DH].bitcast(F32), 0.0))
            chained(pool.memset(v_lo[:, :, :, DH:2 * DH].bitcast(F32), 0.0))
            for name in ORDER[1:]:
                if included("prologue", name):
                    stage("prologue", -1, name)
                if name == "mix2":
                    pool.wait_ge(u_loaded, 16)
                    pool.tensor_copy(u_sb[:, :], u_in[:, :]).then_inc(u_s, 1)
            pool.wait_ge(wv_lo_s, 2)
            run_steps(pool, step, lambda: stage("tail", B, "yst'"))

        @block.scalar
        def _(act):
            def l0_scratch(section, c, name):
                bank, ready, _ = use(section, name, c - 1)
                act.wait_ge(scr_ready, ready)
                return scr[bank], scr_free[bank]

            def mix_tanh(section, c):
                ps, free = l0_scratch(section, c, "mixin")
                act.activation(xxx[:, :], ps[:, 0:T], ACT.Tanh)
                act.activation(xxx4[:, :], ps[0:XM, T:2 * T], ACT.Tanh).then_inc(free, 1)

            def decay_tanh(section, c):
                ps, free = l0_scratch(section, c, "dec1")
                act.activation(dtanh, ps[0:XD, 0:T], ACT.Tanh).then_inc(free, 1)

            def decay_exp(section, c):
                ps, free = l0_scratch(section, c, "dec2")
                for t in range(ET):
                    last = act.activation(w_sb[:, t, :], ps[:, t * T:(t + 1) * T], ACT.Exp, bias=col("decay", t))
                last.then_inc(free, 1)
                _, _, before = use(section, "dec2", c - 1)
                act.wait_ge(free, before + 1)
                act.activation(w_sb[:, :, :], w_sb[:, :, :], ACT.Exp, scale=-1.0).then_inc(w_s, 1)

            def key_receptance(section, c):
                ps, free = l0_scratch(section, c, "kr")
                act.activation(kr_sb[:, :, :, :], ps[:, :].rearrange("p (a t n) -> p a t n", a=2, t=ET),
                               ACT.Copy).then_inc(free, 1)

            def value_gate(section, c):
                ps, free = l0_scratch(section, c, "vg")
                g = ps[:, E:2 * E].rearrange("p (t n) -> p t n", t=ET)
                act.activation(v_sb[:, :], ps[:, 0:E], ACT.Copy).then_inc(v_s, 1)
                act.activation(g_sb[:, :, :], g, ACT.Copy)
                act.activation(gate[:, :, :], g, ACT.Tanh, scale=0.5).then_inc(free, 1)
                act.wait_ge(v_s, c + 1)
                for n in range(4):
                    dst, src = spread_v(n)
                    act.activation(dst, src, ACT.Copy).then_inc(vrep_s, 1)

            def norm_affine(section, c):
                ps, free = l0_scratch(section, c, "attT")
                for t in range(ET):
                    last = act.activation(yT[:, t, :], ps[:, t * T:(t + 1) * T], ACT.Identity,
                                          scale=col("gn_w", t), bias=col("gn_b", t))
                last.then_inc(free, 1)

            def ffn_act(section, c):
                ps, free = l0_scratch(section, c, "kkrr")
                act.activation(ksq[:, :, :], ps[:, 0:E].rearrange("p (t n) -> p t n", t=ET),
                               ACT.Relu).then_inc(relu_s, 1)
                act.activation(rtanh[:, :], ps[:, E:2 * E], ACT.Tanh, scale=0.5).then_inc(free, 1)

            def qk_out(g, p):
                par = p % 2
                act.wait_ge(proj_s, NP * g + p + 1)
                act.activation(q_hi[:, par, :], qk_ps[:, 0, :], ACT.Identity, bias=col("q_bias", p))
                act.activation(k_hi[:, par, :], qk_ps[:, 1, :], ACT.Copy, scale=SCALE).then_inc(qk_hi_s, 1)

            def exps(g, p, h):
                par = p % 2
                act.wait_ge(max_s, 16 * g + 2 * p + h + 1)
                for it in range(ET):
                    last = act.activation(prob[:, par, h, it, :], s_ps[h][:, it, :], ACT.Exp,
                                          bias=nmax[:, par, h, it:it + 1], accum_out=prob_sum[:, par, h, it:it + 1])
                last.then_inc(prob_s, 1)

            def turned(b, p):
                for h in range(2):
                    act.wait_ge(turn_s, 16 * b + (2 * p + h + 1))
                    act.activation(probT_hi[:, p % 2, h, :, :], t_ps[h][:, :, :], ACT.Copy).then_inc(probT_hi_s, 1)

            def attended(section, b, p):
                act.wait_ge(pv_s, NP * b + (p + 1))
                if p == 0 and section != "first":
                    act.wait_ge(scr_ready, use(section, "Y'", b)[1])
                act.activation(attnT[:, p, :], o_ps[:, :], ACT.Copy).then_inc(attn_s, 1)

            def by_pair(ps):
                return ps[:, :].rearrange("p (n h d) -> p n h d", n=4, h=2)

            def values(section, b, name):
                bank, ready, _ = use(section, name, b)
                act.wait_ge(scr_ready, ready)
                oh, lt = int(name[1]), int(name[2])
                act.activation(pair_values(v_hi, oh, lt), by_pair(scr[bank]), ACT.Copy).then_inc(v_hi_s, 1)

            def stage(section, b, name):
                parts = {"mixin": mix_tanh, "dec1": decay_tanh, "dec2": decay_exp, "kr": key_receptance,
                         "vg": value_gate, "attT": norm_affine, "kkrr": ffn_act}
                if name in parts:
                    parts[name](section, b + 1)
                if name.startswith("V"):
                    values(section, b, name)
                if name == "YT'":
                    bank, ready, _ = use(section, name, b)
                    act.wait_ge(scr_ready, ready)
                    act.activation(y_sb[:, :], scr[bank][:, 0:E], ACT.Copy).then_inc(scr_free[bank], 1)
                if name == "split":
                    act.wait_ge(z_s, b + 1)
                    act.activation(zu_hi[:, 0, :], z_sb[:, :], ACT.Copy)
                    act.wait_ge(u_s, b + 1)
                    act.activation(zu_hi[:, 1, :], u_sb[:, :], ACT.Copy).then_inc(zu_hi_s, 1)

            def step(section, b):
                if section != "first":
                    turned(b - 1, NP - 1)
                    attended(section, b - 1, NP - 2)
                qk_out(b, 0)
                if section != "first":
                    attended(section, b - 1, NP - 1)
                for p in range(NP):
                    exps(b, p, 0)
                    exps(b, p, 1)
                    for name in stages(section, p, "a"):
                        stage(section, b, name)
                    if p < NP - 1:
                        qk_out(b, p + 1)
                    if p > 0:
                        turned(b, p - 1)
                    for name in stages(section, p, "b"):
                        stage(section, b, name)
                    if p > 1:
                        attended(section, b, p - 2)
                    for name in stages(section, p, "c"):
                        stage(section, b, name)

            act.wait_ge(setup, 1)
            act.activation(warm[:, :], carrier[:, 0:1], ACT.Exp)
            act.wait_ge(in_cst, 16)
            for name in ORDER:
                if included("prologue", name):
                    stage("prologue", -1, name)
                if name == "vg":
                    act.wait_ge(in_wv0, 16)
                    act.activation(wv_hi[:, 0, :, :], wv_in[0], ACT.Copy).then_inc(wv_hi_s, 1)
                if name == "attT":
                    act.wait_ge(in_wv1, 16)
                    act.activation(wv_hi[:, 1, :, :], wv_in[1], ACT.Copy).then_inc(wv_hi_s, 1)
            act.wait_ge(wv_lo_s, 2)

            def tail():
                turned(B - 1, NP - 1)
                attended("tail", B - 1, NP - 2)
                attended("tail", B - 1, NP - 1)
                stage("tail", B, "YT'")

            run_steps(act, step, tail)

        @block.vector
        def _(dve):
            def wait_apart(s, val):
                dve.wait_ge(s, val)
                dve.tensor_copy(carrier[:, 1:2], carrier[:, 0:1])

            def scratch(section, b, name):
                bank, ready, _ = use(section, name, b)
                dve.wait_ge(scr_ready, ready)
                return scr[bank], scr_free[bank]

            def layer_stats(src, wait, val, st, mv, st_sem, mv_sem, n):
                dve.wait_ge(wait, val)
                dve.bn_stats(st, src).then_inc(st_sem, 1)
                wait_apart(st_sem, n)
                dve.bn_aggr(mv, st).then_inc(mv_sem, 1)

            def normalise(dst, src, mv, rstd, wait, n, ready):
                dve.wait_ge(wait, n)
                dve.tensor_scalar(dst, src, mv[:, 0:1], rstd[:, 0:1], ALU.subtract, ALU.mult).then_inc(ready, 1)

            def shift_in(section, c, name, dst, ln, prev, diff, diff_sem):
                ps, free = scratch(section, c - 1, name)
                for t in range(ET):
                    last = dve.tensor_scalar(dst[:, t, 1:T + 1], ps[:, t * T:(t + 1) * T],
                                             col(ln + "_w", t), col(ln + "_b", t), ALU.mult, ALU.add)
                last.then_inc(free, 1)
                dve.wait_ge(prev, c + 1)
                dve.wait_ge(free, use(section, name, c - 1)[2] + 1)
                dve.tensor_tensor(diff[:, :, :], dst[:, :, 0:T], dst[:, :, 1:T + 1], ALU.subtract).then_inc(diff_sem, 1)
                dve.wait_ge(diff_sem, c + 1)

            def mix_in(c):
                for t in range(ET):
                    last = dve.scalar_tensor_tensor(xin[:, t, :], sx[:, t, :], col("maa_x", t), xn[:, t, 1:T + 1],
                                                    ALU.mult, ALU.add)
                last.then_inc(xin_s, 1)

            def mixes(section, c, n):
                name, slots = MIX_USES[n]
                ps, free = scratch(section, c - 1, name)
                for k, slot in enumerate(slots):
                    for t in range(ET):
                        last = dve.scalar_tensor_tensor(
                            x5[:, slot, t, :], ps[:, (k * ET + t) * T:(k * ET + t + 1) * T],
                            col("maa", MIX_ORDER[slot] * ET + t), sx[:, t, :], ALU.add, ALU.mult)
                last.then_inc(free, 1)

            def bonus_rk(section, c):
                bank, _, before = use(section, "kr", c - 1)
                dve.wait_ge(scr_free[bank], before + 1)
                for t in range(ET):
                    last = dve.scalar_tensor_tensor(bonus[:, t, :], kr_sb[:, 1, t, :], col("bonus", t),
                                                    kr_sb[:, 0, t, :], ALU.mult, ALU.mult)
                last.then_inc(bonus_s, 1)

            def make_gate(section, c):
                bank, _, before = use(section, "vg", c - 1)
                dve.wait_ge(scr_free[bank], before + 1)
                dve.scalar_tensor_tensor(gate[:, :, :], gate[:, :, :], 1.0, g_sb[:, :, :],
                                         ALU.add, ALU.mult).then_inc(gate_s, 1)

            def key_value(section, c, n):
                t, dh = n // 2, n % 2
                ps, free = scratch(section, c - 1, f"vr{n}")
                k = kr_sb[:, 0, t:t + 1, :].to_broadcast([P, 4, T])
                dve.tensor_tensor(kv[:, n, :, :], ps[:, :].rearrange("p (d n) -> p d n", d=4), k,
                                  ALU.mult).then_inc(free, 1)

            def scans(section, c, n):
                t, dh = n // 2, n % 2
                bank, _, before = use(section, f"vr{n}", c - 1)
                dve.wait_ge(scr_free[bank], before + 1)
                if n == 0:
                    dve.wait_ge(w_s, c + 1)
                    dve.wait_ge(s0_s, c + 1)
                for d in range(dh * 4, dh * 4 + 4):
                    last = dve.tensor_tensor_scan(states[:, t, d, 1:T + 1], w_sb[:, t, :], kv[:, n, d - dh * 4, :],
                                                  states[:, t, d, 0:1], ALU.mult, ALU.add)
                last.then_inc(scan_s, 1)

            def heads(a):
                return a.rearrange("p (h d) -> p h d", d=SD)

            def spread(a):
                return a.rearrange("p (h o) -> p h o", o=1).to_broadcast([P, HT, SD])

            def group_norm(section, c, t):
                name = f"red{t}"
                ps, free = scratch(section, c - 1, name)
                n = 14 * c + 7 * t
                ch = slice(t * P, (t + 1) * P)
                y, cent, tmp = heads(att[:, ch]), heads(xhat[:, ch]), bonus_v[:, ch]
                dve.tensor_tensor(heads(tmp), heads(v_sb[:, ch]), spread(ps[:, P:P + HT]), ALU.mult).then_inc(gn_s, 1)
                dve.wait_ge(gn_s, n + 1)
                dve.tensor_tensor(att[:, ch], ps[:, 0:P], tmp, ALU.add).then_inc(free, 1)
                dve.wait_ge(free, use(section, name, c - 1)[2] + 1)
                dve.tensor_reduce(hsum[:, t, :], y, AX.X, ALU.add).then_inc(gn_s, 1)
                dve.wait_ge(gn_s, n + 2)
                dve.scalar_tensor_tensor(cent, spread(hsum[:, t, :]), -1.0 / SD, y, ALU.mult, ALU.add).then_inc(gn_s, 1)
                dve.wait_ge(gn_s, n + 3)
                dve.tensor_tensor(tmp, xhat[:, ch], xhat[:, ch], ALU.mult).then_inc(gn_s, 1)
                dve.wait_ge(gn_s, n + 4)
                dve.tensor_reduce(hsq[:, t, :], heads(tmp), AX.X, ALU.add).then_inc(gn_s, 1)
                dve.wait_ge(gn_s, n + 5)
                dve.tensor_scalar(hve[:, t, :], hsq[:, t, :], 1.0 / SD, EPS, ALU.mult, ALU.add).then_inc(gn_s, 2)

            def group_normed(c, t):
                ch = slice(t * P, (t + 1) * P)
                dve.wait_ge(hrstd_s, 2 * c + t + 1)
                dve.tensor_tensor(heads(att[:, ch]), heads(xhat[:, ch]), spread(hrstd[:, t, :]),
                                  ALU.mult).then_inc(yhat_s, 1)

            def gated(section, c):
                bank, _, before = use(section, "attT", c - 1)
                dve.wait_ge(scr_free[bank], before + 1)
                dve.scalar_tensor_tensor(ygT, gate[:, :, :], 0.5, yT, ALU.mult,
                                         ALU.mult).then_inc(ygT_s, 1)

            def residual1(section, c):
                ps, free = scratch(section, c - 1, "wo")
                dve.tensor_tensor(x1[:, :], ps[:, 0:E], x_sb[:, :], ALU.add).then_inc(free, 1)
                layer_stats(x1[:, :], free, use(section, "wo", c - 1)[2] + 1, st2[:, :], mv2[:, :],
                            stats2, mean2, c + 1)

            def residual1_normed(c):
                normalise(xhat[:, :], x1[:, :], mv2, rstd2, rstd2_s, c + 1, xhat2_s)

            def ffn_in(section, c):
                shift_in(section, c, "x2T", xn2, "ln2", prev2_s, sx2, sx2_s)
                for dst, name in ((xk, "ffn_k"), (xr, "ffn_r")):
                    for t in range(ET):
                        last = dve.scalar_tensor_tensor(dst[:, t, :], sx2[:, t, :], col(name, t),
                                                        xn2[:, t, 1:T + 1], ALU.mult, ALU.add)
                last.then_inc(xkr_s, 1)

            def ffn_mid(section, c):
                dve.wait_ge(relu_s, c + 1)
                dve.tensor_tensor(ksq[:, :, :], ksq[:, :, :], ksq[:, :, :], ALU.mult).then_inc(ksq_s, 1)

            def make_z(section, c):
                ps, free = scratch(section, c - 1, "ffn")
                bank, _, before = use(section, "kkrr", c - 1)
                dve.wait_ge(scr_free[bank], before + 1)
                dve.scalar_tensor_tensor(rtanh[:, :], rtanh[:, :], 1.0, ps[:, 0:E], ALU.add, ALU.mult).then_inc(free, 1)
                dve.wait_ge(free, use(section, "ffn", c - 1)[2] + 1)
                if section != "prologue":
                    dve.wait_ge(proj_s, NP * c)
                    dve.wait_ge(zres_s, c)
                dve.scalar_tensor_tensor(z_sb[:, :], rtanh[:, :], 0.5, x1[:, :], ALU.mult, ALU.add).then_inc(z_s, 1)

            def qk_out(g, p):
                par = p % 2
                dve.wait_ge(qk_hi_s, NP * g + p + 1)
                dve.scalar_tensor_tensor(q_lo[:, par, :], qk_ps[:, 0, :], col("q_bias", p), q_hi[:, par, :], ALU.add,
                                         ALU.subtract)
                dve.scalar_tensor_tensor(k_lo[:, par, :], qk_ps[:, 1, :], SCALE, k_hi[:, par, :], ALU.mult,
                                         ALU.subtract).then_inc(qk_s, 1)

            def maxes(b, p, h):
                dve.wait_ge(score_s, 16 * b + 2 * p + h + 1)
                dve.tensor_reduce(nmax[:, p % 2, h, :], s_ps[h][:, :, :], AX.X, ALU.max, negate=True).then_inc(max_s, 1)

            def turned(b, p):
                for h in range(2):
                    dve.wait_ge(probT_hi_s, 16 * b + (2 * p + h + 1))
                    dve.tensor_tensor(probT_lo[:, p % 2, h, :, :], t_ps[h][:, :, :], probT_hi[:, p % 2, h, :, :],
                                      ALU.subtract).then_inc(probT_s, 1)

            def sums(b, p):
                dve.wait_ge(prob_s, 16 * b + (2 * p + 2))
                dve.reciprocal(rden[:, p % 2, :, :], prob_sum[:, p % 2, :, :]).then_inc(rden_s, 1)

            def values(section, b, name):
                bank, _, _ = use(section, name, b)
                oh, lt = int(name[1]), int(name[2])
                dve.wait_ge(v_hi_s, 4 * b + (2 * oh + lt + 1))
                ps = scr[bank][:, :].rearrange("p (n h d) -> p n h d", n=4, h=2)
                dve.tensor_tensor(pair_values(v_lo, oh, lt), ps, pair_values(v_hi, oh, lt),
                                  ALU.subtract).then_inc(scr_free[bank], 1)

            def add_z(section, b):
                ps, free = scratch(section, b, "Y'")
                dve.wait_ge(zres_s, b)
                dve.tensor_tensor(y_sb[:, :], ps[:, 0:E], zres[:, :], ALU.add).then_inc(free, 1)
                dve.wait_ge(free, use(section, "Y'", b)[2] + 1)
                dve.tensor_copy(carrier[:, 1:2], carrier[:, 0:1]).then_inc(y_s, 1)

            def finish(section, b):
                bank, _, before = use(section, "YT'", b)
                dve.wait_ge(scr_free[bank], before + 1)
                for t in range(ET):
                    last = dve.bn_stats(st3[:, t, :], yn[:, t, :])
                    last.then_inc(stats3, 1)
                wait_apart(stats3, 2 * b)
                for t in range(ET):
                    last = dve.bn_aggr(mv3[:, t, :], st3[:, t, :])
                last.then_inc(mean3, 1)

            def finish_normed(section, b):
                dve.wait_ge(rstd3_s, b)
                for t in range(ET):
                    last = dve.tensor_scalar(yn[:, t, :], yn[:, t, :], mv3[:, t, 0:1], rstd3[:, t:t + 1],
                                             ALU.subtract, ALU.mult)
                last.then_inc(yn_s, 1)

            def store_out(section, b):
                ps, free = scratch(section, b, "OT'")
                if section == "tail":
                    dve.wait_ge(out_stored, 16 * (b - 1))
                dve.tensor_copy(o_sb[:, :], ps[:, 0:E]).then_inc(free, 1)

            def stage(section, b, name):
                c = b + 1
                if name == "ln1":
                    layer_stats(x_sb[:, :], x_in, 16 * (c + 1), st1[:, :], mv1[:, :], stats1, mean1, c + 1)
                if name == "xhat":
                    normalise(xhat[:, :], x_sb[:, :], mv1, rstd1, rstd1_s, c + 1, xhat_s)
                if name == "xT":
                    shift_in(section, c, "xT", xn, "ln1", prev1_s, sx, sx_s)
                    mix_in(c)
                if name in ("mix0", "mix1", "mix2"):
                    mixes(section, c, int(name[3]))
                if name == "vg":
                    bonus_rk(section, c)
                    make_gate(section, c)
                if name in ("vr0", "vr1", "vr2", "vr3"):
                    key_value(section, c, int(name[2]))
                if name in ("scan0", "scan1", "scan2", "scan3"):
                    scans(section, c, int(name[4]))
                if name in ("red0", "red1"):
                    group_norm(section, c, int(name[3]))
                if name in ("hrstd0", "hrstd1"):
                    group_normed(c, int(name[5]))
                if name == "attT":
                    gated(section, c)
                if name == "wo":
                    residual1(section, c)
                if name == "xhat2":
                    residual1_normed(c)
                if name == "x2T":
                    ffn_in(section, c)
                if name == "kkrr":
                    ffn_mid(section, c)
                if name == "ffn":
                    make_z(section, c)
                if name.startswith("V"):
                    values(section, b, name)
                if name == "Y'":
                    add_z(section, b)
                if name == "yst'":
                    finish(section, b)
                if name == "yn'":
                    finish_normed(section, b)
                if name == "OT'":
                    store_out(section, b)

            def step(section, b):
                if included(section, "ln1"):
                    stage(section, b, "ln1")
                if section != "first":
                    turned(b - 1, NP - 1)
                if included(section, "xhat"):
                    stage(section, b, "xhat")
                qk_out(b, 0)
                if included(section, "xT"):
                    stage(section, b, "xT")
                for p in range(NP):
                    maxes(b, p, 0)
                    maxes(b, p, 1)
                    for name in stages(section, p, "a"):
                        stage(section, b, name)
                    sums(b, p)
                    if p < NP - 1:
                        qk_out(b, p + 1)
                    if p > 0:
                        turned(b, p - 1)
                    for name in stages(section, p, "b"):
                        stage(section, b, name)
                    for name in stages(section, p, "c"):
                        stage(section, b, name)
                if section == "loop":
                    dve.wait_ge(out_stored, 16 * b)

            def tail():
                turned(B - 1, NP - 1)
                add_z("tail", B)
                finish("tail", B)
                finish_normed("tail", B)
                store_out("tail", B)

            dve.memset(w2a_sb[:, :, :], 0.0).then_inc(w2a_zeroed, 1)
            dve.wait_ge(in_cst, 16)
            dve.wait_ge(setup, START_STEPS)
            for name in ORDER:
                if included("prologue", name):
                    stage("prologue", -1, name)
                if name in ("red1", "x2T"):
                    n = ("red1", "x2T").index(name)
                    dve.wait_ge(wv_hi_s, n + 1)
                    dve.tensor_tensor(wv_lo[:, n, :, :], wv_in[n], wv_hi[:, n, :, :], ALU.subtract).then_inc(wv_lo_s, 1)
            run_steps(dve, step, tail)

        @block.tensor
        def _(pe):
            def read(section, b, name):
                bank, _, before = use(section, name, b)
                pe.wait_ge(scr_free[bank], before + 1)

            def scratch(section, b, name):
                bank, _, before = use(section, name, b)
                if section != "prologue" or before > 0:
                    pe.wait_ge(scr_free[bank], before)
                return scr[bank]

            def tokens_first(ps, weight, src, col0=0):
                for t in range(ET):
                    last = pe.matmul(ps[:, col0:col0 + E], src[:, t, :], weight[:, t, :],
                                     start=(t == 0), stop=(t == ET - 1))
                return last

            def channels_first(ps, weight, src, col0=0):
                for f in range(ET):
                    for t in range(ET):
                        last = pe.matmul(ps[:, col0 + f * T:col0 + (f + 1) * T], weight[:, t, f * P:(f + 1) * P],
                                         src[:, t, :], start=(t == 0), stop=(t == ET - 1))
                return last

            def turn(ps, src):
                for t in range(ET):
                    last = pe.transpose(ps[:, t * T:(t + 1) * T], src[:, t * P:(t + 1) * P], ident[:, :])
                return last

            def l0_use(section, c, name):
                b = c - 1
                if name == "xT":
                    pe.wait_ge(xhat_s, c + 1)
                    last = turn(scratch(section, b, name), xhat)
                elif name == "mixin":
                    pe.wait_ge(xin_s, c + 1)
                    ps = scratch(section, b, name)
                    for t in range(ET):
                        pe.matmul(ps[:, 0:T], w1_sb[:, t, 0:4 * XM], xin[:, t, :], start=(t == 0), stop=(t == ET - 1))
                    for t in range(ET):
                        last = pe.matmul(ps[0:XM, T:2 * T], w1_sb[:, t, 4 * XM:5 * XM], xin[:, t, :],
                                         start=(t == 0), stop=(t == ET - 1))
                elif name in ("mix0", "mix1", "mix2"):
                    if name == "mix0":
                        read(section, b, "mixin")
                    slots = MIX_USES[int(name[3])][1]
                    ps = scratch(section, b, name)
                    for k, slot in enumerate(slots):
                        m = MIX_ORDER[slot]
                        for t in range(ET):
                            w = w2a_sb[:, m, t * P:(t + 1) * P] if m < 4 else w2b_sb[:, t * P:(t + 1) * P]
                            v = xxx[:, :] if m < 4 else xxx4[:, :]
                            last = pe.matmul(ps[:, (k * ET + t) * T:(k * ET + t + 1) * T], w, v, start=True, stop=True)
                elif name == "dec1":
                    pe.wait_ge(x5_s, 3 * c + 1)
                    ps = scratch(section, b, name)
                    for t in range(ET):
                        last = pe.matmul(ps[0:XD, 0:T], dw1_sb[:, t, :], x5[:, SLOT_W, t, :],
                                         start=(t == 0), stop=(t == ET - 1))
                elif name == "dec2":
                    read(section, b, "dec1")
                    ps = scratch(section, b, name)
                    for t in range(ET):
                        last = pe.matmul(ps[:, t * T:(t + 1) * T], dw2_sb[:, t * P:(t + 1) * P], dtanh,
                                         start=True, stop=True)
                elif name == "kr":
                    pe.wait_ge(x5_s, 3 * c + 2)
                    ps = scratch(section, b, name)
                    channels_first(ps, l0_weight("Wk"), x5[:, SLOT_K])
                    last = channels_first(ps, l0_weight("Wr"), x5[:, SLOT_R], E)
                elif name == "vg":
                    pe.wait_ge(x5_s, 3 * c + 3)
                    ps = scratch(section, b, name)
                    tokens_first(ps, l0_weight("Wv"), x5[:, SLOT_V])
                    last = channels_first(ps, l0_weight("Wg"), x5[:, SLOT_G], E)
                elif name in ("vr0", "vr1", "vr2", "vr3"):
                    n = int(name[2])
                    pe.wait_ge(vrep_s, 4 * c + n + 1)
                    ps = scratch(section, b, name)
                    for d in range(4):
                        last = pe.transpose(ps[:, d * T:(d + 1) * T], vrep[:, n, d, :], ident[:, :])
                elif name in ("red0", "red1"):
                    ps = scratch(section, b, name)
                    pe.wait_ge(bonus_s, c + 1)
                    t = int(name[3])
                    pe.matmul(ps[:, P:P + HT], bonus[:, t, :], head_ones[:, :], start=True, stop=True)
                    for dh in range(2):
                        n = 2 * t + dh
                        pe.wait_ge(rs_s, 4 * c + n + 1)
                        for d in range(dh * 4, dh * 4 + 4):
                            last = pe.matmul(ps[:, 0:P], kv[:, n, d - dh * 4, :], select[:, :, SD - d:2 * SD - d],
                                             start=(d == 0), stop=(d == SD - 1))
                elif name == "attT":
                    pe.wait_ge(yhat_s, 2 * c + 2)
                    last = turn(scratch(section, b, name), att)
                elif name == "wo":
                    pe.wait_ge(ygT_s, c + 1)
                    last = tokens_first(scratch(section, b, name), l0_weight("Wo"), ygT)
                elif name == "x2T":
                    pe.wait_ge(xhat2_s, c + 1)
                    last = turn(scratch(section, b, name), xhat)
                elif name == "kkrr":
                    pe.wait_ge(xkr_s, c + 1)
                    ps = scratch(section, b, name)
                    channels_first(ps, l0_weight("fWk"), xk)
                    last = tokens_first(ps, l0_weight("fWr"), xr, E)
                else:
                    assert name == "ffn", name
                    pe.wait_ge(ksq_s, c + 1)
                    last = tokens_first(scratch(section, b, name), l0_weight("fWv"), ksq)
                last.then_inc(scr_ready, 1)

            def project(b, p):
                n = NP * b + p
                if p == 0:
                    pe.wait_ge(z_s, b + 1)
                    pe.wait_ge(u_s, b + 1)
                if not (isinstance(b, int) and n == 0):
                    pe.wait_ge(qk_s, n)
                for a in range(2):
                    for lt in range(ET):
                        dst = qk_ps[:, a, lt * P:(lt + 1) * P]
                        o = slice(a * HD + p * P, a * HD + (p + 1) * P)
                        pe.matmul(dst, wqk_sb[:, 0, lt, o], z_sb[:, lt * P:(lt + 1) * P], start=True, stop=False)
                        last = pe.matmul(dst, wqk_sb[:, 1, lt, o], u_sb[:, lt * P:(lt + 1) * P], start=False, stop=True)
                last.then_inc(proj_s, 1)

            def values(section, b, name):
                oh, lt = int(name[1]), int(name[2])
                if name == "V00":
                    pe.wait_ge(zu_lo_s, b + 1)
                    if section == "first":
                        pe.wait_ge(wv_lo_s, 2)
                ps = scratch(section, b, name)
                o = slice(oh * (HD // 2), (oh + 1) * (HD // 2))
                terms = [(n, x, w) for n in range(2) for x, w in ((zu_hi, wv_hi), (zu_hi, wv_lo), (zu_lo, wv_hi))]
                for i, (n, x, w) in enumerate(terms):
                    last = pe.matmul(ps[:, :], x[:, n, lt * P:(lt + 1) * P], w[:, n, lt, o], start=(i == 0),
                                     stop=(i == len(terms) - 1))
                last.then_inc(scr_ready, 1)

            def scores(section, b, p):
                pe.wait_ge(qk_s, NP * b + (p + 1))
                for h in range(2):
                    if p > 0 or section != "first":
                        pe.wait_ge(prob_s, 16 * b + (2 * p + h - 1))
                    rows = slice(h * DH, (h + 1) * DH)
                    for it in range(ET):
                        for i, (q, k) in enumerate(((q_hi, k_hi), (q_hi, k_lo), (q_lo, k_hi))):
                            last = pe.matmul(s_ps[h][:, it, :], q[rows, p % 2, it * P:(it + 1) * P], k[rows, p % 2, :],
                                             start=(i == 0), stop=(i == 2))
                    last.then_inc(score_s, 1)

            def turn_probs(first, b, p):
                for h in range(2):
                    pe.wait_ge(norm_s, 16 * b + (2 * p + h + 1))
                    if not first:
                        pe.wait_ge(probT_s, 16 * b + (2 * p + h - 1))
                    for it in range(ET):
                        for jt in range(ET):
                            last = pe.transpose(t_ps[h][:, jt, it * P:(it + 1) * P],
                                                prob[:, p % 2, h, it, jt * P:(jt + 1) * P],
                                                ident[:, :])
                    last.then_inc(turn_s, 1)

            def attend(first, b, p):
                if not first:
                    pe.wait_ge(attn_s, NP * b + p)
                pe.wait_ge(probT_s, 16 * b + (2 * p + 2))
                terms = [(h, jt, v, pr) for h in range(2) for jt in range(ET)
                         for v, pr in ((v_hi, probT_hi), (v_lo, probT_hi), (v_hi, probT_lo))]
                for i, (h, jt, v, pr) in enumerate(terms):
                    last = pe.matmul(o_ps[:, :], v[:, jt, p, h * DH:(h + 2) * DH], pr[:, p % 2, h, jt, :],
                                     start=(i == 0), stop=(i == len(terms) - 1))
                last.then_inc(pv_s, 1)

            def output(section, b, pairs=range(NP)):
                ps = scratch(section, b, "Y'") if 0 in pairs else scr[use(section, "Y'", b)[0]]
                for p in pairs:
                    pe.wait_ge(attn_s, NP * b + (p + 1 - NP))
                    last = pe.matmul(ps[:, 0:E], wo1_sb[:, p, :], attnT[:, p, :], start=(p == 0), stop=(p == NP - 1))
                if NP - 1 in pairs:
                    last.then_inc(scr_ready, 1)

            def output_to_rows(section, b):
                pe.wait_ge(y_s, b)
                turn(scratch(section, b, "YT'"), y_sb).then_inc(scr_ready, 1)

            def output_turned(section, b):
                pe.wait_ge(yn_s, b)
                ps = scratch(section, b, "OT'")
                for t in range(ET):
                    last = pe.transpose(ps[:, t * P:(t + 1) * P], yn[:, t, :], ident[:, :])
                last.then_inc(scr_ready, 1)

            def stage(section, b, name):
                if name in NO_SCRATCH:
                    return
                if name.startswith("V"):
                    values(section, b, name)
                elif name == "Y'":
                    output(section, b)
                elif name == "YT'":
                    output_to_rows(section, b)
                elif name == "OT'":
                    output_turned(section, b)
                else:
                    l0_use(section, b + 1, name)

            def step(section, b):
                if section != "first":
                    turn_probs(False, b - 1, NP - 1)
                    attend(False, b - 1, NP - 2)
                project(b, 0)
                if included(section, "xT"):
                    stage(section, b, "xT")
                if section != "first":
                    attend(False, b - 1, NP - 1)
                for p in range(NP):
                    scores(section, b, p)
                    for name in stages(section, p, "a"):
                        stage(section, b, name)
                    if p < NP - 1:
                        project(b, p + 1)
                    if p > 0:
                        turn_probs(section == "first" and p == 1, b, p - 1)
                    for name in stages(section, p, "b"):
                        stage(section, b, name)
                    if p > 1:
                        attend_values(section, b, p - 2)
                        attend(section == "first" and p == 2, b, p - 2)
                    for name in stages(section, p, "c"):
                        stage(section, b, name)

            def attend_values(section, b, p):
                if p in (0, 4):
                    read(section, b, f"V{p // 4}0")
                    read(section, b, f"V{p // 4}1")

            def tail():
                turn_probs(False, B - 1, NP - 1)
                attend(False, B - 1, NP - 2)
                output("tail", B, range(NP - 2))
                attend(False, B - 1, NP - 1)
                output("tail", B, range(NP - 2, NP))
                output_to_rows("tail", B)
                output_turned("tail", B)

            pe.wait_ge(setup, START_STEPS)
            for name in L0_USES:
                for _ in range(FILL.get(name, 0)):
                    pe.matmul(o_ps[:, 0:P], ident[:, :], ident[:, :], start=True, stop=True)
                if name == "mixin":
                    pe.wait_ge(in_mix, 16 * 6)
                if name == "dec1":
                    pe.wait_ge(in_l0a, 16 * 3)
                if name == "red0":
                    pe.wait_ge(setup, SETUP_STEPS)
                if name == "wo":
                    pe.wait_ge(in_l0b, 16)
                stage("prologue", -1, name)
            pe.wait_ge(in_l1a, 32)
            pe.wait_ge(in_wo1, 16)
            run_steps(pe, step, tail)
    return nc


def kernel(**inputs):
    import numpy as np
    import concourse.bacc as bacc
    from concourse.bass_utils import run_bass_kernel_spmd

    a = {k: np.asarray(v) for k, v in inputs.items()}
    l0 = {k[len("L0_xattn_"):]: v for k, v in a.items() if k.startswith("L0_xattn_")}
    l1 = {k[len("L1_xattn_"):]: v for k, v in a.items() if k.startswith("L1_xattn_")}

    def tiles(v):
        v = v.reshape(-1, ET, P)
        return np.moveaxis(v, 2, 0).reshape(P, -1)

    def rows(w):
        return np.moveaxis(w.reshape(ET, P, -1), 1, 0)

    parts = {
        "ln1_w": l0["ln1_w"], "ln1_b": l0["ln1_b"], "ln2_w": l0["ln2_w"], "ln2_b": l0["ln2_b"],
        "maa_x": l0["maa_x"], "maa": l0["maa_stack"], "decay": l0["time_decay"], "bonus": l0["faaaa"].reshape(E),
        "gn_w": l0["gn_w"], "gn_b": l0["gn_b"], "ffn_k": l0["ffn_maa_k"], "ffn_r": l0["ffn_maa_r"],
    }
    laid = {k: tiles(v) for k, v in parts.items()}
    laid["bo"] = l1["bo"].reshape(P, 1)
    laid["q_bias"] = l1["r_w_bias"].reshape(NP, P).T
    ctx_np = a["ctx_2048"]
    laid["prev"] = tiles(np.stack([ctx_np[:, 1, :], ctx_np[:, 0, :]]))
    arrays = {
        "x": a["x"],
        "ctx_in": ctx_np,
        "consts": np.concatenate([laid[name] for name, _ in CONSTS], axis=1),
        "state0": np.moveaxis(ctx_np[:, 2:2 + SD, :].reshape(B, ET, P, SD), 2, 0),
        "l0w": np.stack([rows(l0[n].T) for n in
                         ("Wk", "Wr", "Wv", "Wg", "Wo", "ffn_Wk", "ffn_Wr", "ffn_Wv")], axis=1),
        "maa_w1": rows(l0["maa_w1"]),
        "maa_w2": l0["maa_w2"].reshape(MIX * XM, E),
        "decay_w1": rows(l0["decay_w1"]),
        "decay_w2": l0["decay_w2"],
        "wqkv": np.stack([l1["Wqkv0"].T, l1["Wqkv1"].T], axis=1),
        "winj": np.stack([l1["Winj0"].T, l1["Winj1"].T], axis=1),
        "wo1": np.moveaxis(l1["Wo"].T.reshape(NP, P, P), 1, 0),
    }
    arrays = {f"in_{k}": np.ascontiguousarray(v) for k, v in arrays.items()}
    nc = bacc.Bacc("TRN2", target_bir_lowering=False, num_devices=1)
    args = [nc.dram_tensor(k, v.shape, mybir.dt.from_np(v.dtype), kind="ExternalInput").ap() for k, v in arrays.items()]
    args.append(nc.dram_tensor("out_z", (B, T, E), F32, kind="ExternalOutput").ap())
    rwkv_then_attention(nc, *args)
    r = run_bass_kernel_spmd(nc, [arrays], core_ids=[0])
    return r.results[0]["out_z"]
```
